# Optimizing a Trainium2 kernel written in Bass

```python
import numpy as np
import jax
import jax.numpy as jnp

def _softmax(x, axis=-1):
    return jax.nn.softmax(x, axis=axis)

def _gelu(x):
    return jax.nn.gelu(x, approximate=True)

def _silu(x):
    return jax.nn.silu(x)

def _sigmoid(x):
    return jax.nn.sigmoid(x)

def _layernorm(x, axis=-1, eps=1e-05):
    m = jnp.mean(x, axis=axis, keepdims=True)
    v = jnp.var(x, axis=axis, keepdims=True)
    return (x - m) / jnp.sqrt(v + eps)

def _scatter_add(tgt, idx, src, axis=0):
    return tgt.at[idx].add(src)

def _segment_sum(src, seg, n):
    return jax.ops.segment_sum(src, seg, n)
kernel_name = 'mk_early_fusion_embed_d1_tok_img768_r4_368948'

def setup_inputs(seed: int=0):
    np.random.seed(seed)
    _w = jnp.asarray

    def _rec_inputs():
        import jax
        import jax.numpy as jnp
        _rk = jax.random.key(seed)
        x = jax.random.uniform(jax.random.fold_in(_rk, 1), (4, 3, 224, 224), jnp.float32, 0.0, 0.001)
        x_txt = jax.random.randint(jax.random.fold_in(_rk, 51), (4, 512), 0, 127999, jnp.int32)
        return (x, x_txt)
    x, x_txt = _rec_inputs()

    def _L0_tok_setup():
        import jax, jax.numpy as jnp
        import numpy as np
        C_CURV = 1.0
        EPS = 1e-15
        BALL_EPS = 0.004

        def _artanh(x):
            x = jnp.clip(x, -1.0 + 1e-07, 1.0 - 1e-07)
            return jnp.arctanh(x)

        def _project(x):
            norm = jnp.maximum(jnp.linalg.norm(x, axis=-1, keepdims=True), EPS)
            maxnorm = (1.0 - BALL_EPS) / jnp.sqrt(C_CURV)
            return jnp.where(norm > maxnorm, x / norm * maxnorm, x)

        def _mobius_matvec(W, x):
            sqrt_c = jnp.sqrt(C_CURV)
            x_norm = jnp.maximum(jnp.linalg.norm(x, axis=-1, keepdims=True), EPS)
            mx = x @ W.T
            mx_norm = jnp.maximum(jnp.linalg.norm(mx, axis=-1, keepdims=True), EPS)
            res = jnp.tanh(mx_norm / x_norm * _artanh(sqrt_c * x_norm)) * mx / (mx_norm * sqrt_c)
            zero_row = jnp.all(mx == 0, axis=-1, keepdims=True)
            res = jnp.where(zero_row, jnp.zeros_like(res), res)
            return _project(res)

        def _mobius_add(x, y):
            c = C_CURV
            x2 = jnp.sum(x * x, axis=-1, keepdims=True)
            y2 = jnp.sum(y * y, axis=-1, keepdims=True)
            xy = jnp.sum(x * y, axis=-1, keepdims=True)
            num = (1.0 + 2.0 * c * xy + c * y2) * x + (1.0 - c * x2) * y
            denom = jnp.maximum(1.0 + 2.0 * c * xy + c * c * x2 * y2, EPS)
            return _project(num / denom)

        def _patchify(x, p):
            B, C, H, W = x.shape
            hp, wp = (H // p, W // p)
            x = x.reshape(B, C, hp, p, wp, p)
            x = x.transpose(0, 2, 4, 1, 3, 5)
            return x.reshape(B, hp * wp, C * p * p)
        key = jax.random.key(seed)
        k1, k2, k3 = jax.random.split(key, 3)
        B, C, H = (64, 3, 224)
        p, D = (16, 192)
        patch_dim = C * p * p
        x = jax.random.uniform(k1, (B, C, H, H), dtype=jnp.float32) * 0.001
        bound_w = 1.0 / np.sqrt(patch_dim)
        W = jax.random.uniform(k2, (D, patch_dim), dtype=jnp.float32, minval=-bound_w, maxval=bound_w)
        bound_b = 1.0 / np.sqrt(patch_dim)
        b = jax.random.uniform(k3, (D,), dtype=jnp.float32, minval=-bound_b, maxval=bound_b) * 0.01
        return {'x': x, 'W': W, 'b': b}
    _L0_tok_all = _L0_tok_setup()
    _L0_tok_in = {k: v for k, v in _L0_tok_all.items() if k in ('W', 'b')}
    del _L0_tok_all

    def _L0_txt_setup():
        import jax, jax.numpy as jnp
        import numpy as np
        import math
        VOCAB = 32000
        BASIN_DIM = 64
        D_MODEL = 192
        EPS = 1e-08
        key = jax.random.key(seed)
        k1, k2, k3, k4 = jax.random.split(key, 4)
        token_ids = jax.random.randint(k1, (8, 1024), 0, VOCAB, dtype=jnp.int32)
        coords = jax.random.normal(k2, (VOCAB, BASIN_DIM), dtype=jnp.float32)
        coords = coords / jnp.linalg.norm(coords, axis=-1, keepdims=True)
        coords = coords * (math.sqrt(BASIN_DIM) / 5.0)
        coords = coords + jax.random.normal(k3, coords.shape, dtype=jnp.float32) * 0.01
        w = jax.random.normal(k4, (D_MODEL, BASIN_DIM), dtype=jnp.float32)
        q, _ = jnp.linalg.qr(w)
        proj_w = q * 0.1
        norm_w = jnp.ones((D_MODEL,), dtype=jnp.float32)
        return {'token_ids': token_ids, 'basin_coords': coords, 'proj_w': proj_w, 'norm_w': norm_w}
    _L0_txt_all = _L0_txt_setup()
    _L0_txt_in = {k: v for k, v in _L0_txt_all.items() if k in ('basin_coords', 'proj_w', 'norm_w')}
    del _L0_txt_all

    def _L0_attn_setup():
        import jax, jax.numpy as jnp
        import numpy as np
        import math
        N_LAYER, N_EMBD, LAYER_ID = (12, 192, 0)
        B, T, C = (32, 256, N_EMBD)

        def _init_params():
            r01 = LAYER_ID / (N_LAYER - 1)
            r1a0 = 1.0 - LAYER_ID / N_LAYER
            h = np.arange(C, dtype=np.float32)
            time_decay = (-5.0 + 8.0 * (h / (C - 1)) ** (0.7 + 1.3 * r01)).astype(np.float32)
            zigzag = np.array([(i + 1) % 3 - 1 for i in range(C)], dtype=np.float32) * 0.5
            time_first = (np.ones(C, dtype=np.float32) * math.log(0.3) + zigzag).astype(np.float32)
            xlin = (np.arange(C, dtype=np.float32) / C).reshape(1, 1, C)
            time_mix_k = np.power(xlin, r1a0).astype(np.float32)
            time_mix_v = (np.power(xlin, r1a0) + 0.3 * r01).astype(np.float32)
            time_mix_r = np.power(xlin, 0.5 * r1a0).astype(np.float32)
            return (time_decay, time_first, time_mix_k, time_mix_v, time_mix_r)

        def _wkv(w, u, k, v):

            def step(carry, kv):
                p, q, o = carry
                kt, vt = kv
                no = jnp.maximum(o, u + kt)
                A = jnp.exp(o - no)
                Bc = jnp.exp(u + kt - no)
                y = (A * p + Bc * vt) / (A * q + Bc)
                no2 = jnp.maximum(w + o, kt)
                A2 = jnp.exp(w + o - no2)
                B2 = jnp.exp(kt - no2)
                return ((A2 * p + B2 * vt, A2 * q + B2, no2), y)
            b = k.shape[0]
            init = (jnp.zeros((b, C), jnp.float32), jnp.zeros((b, C), jnp.float32), jnp.full((b, C), -1e+38, jnp.float32))
            kT = jnp.swapaxes(k, 0, 1)
            vT = jnp.swapaxes(v, 0, 1)
            _, ys = jax.lax.scan(step, init, (kT, vT))
            return jnp.swapaxes(ys, 0, 1)
        key = jax.random.key(seed)
        ks = jax.random.split(key, 5)
        td, tf, tmk, tmv, tmr = _init_params()
        scale = 0.02
        return {'x': jax.random.normal(ks[0], (B, T, C), dtype=jnp.float32), 'time_decay': jnp.asarray(td), 'time_first': jnp.asarray(tf), 'time_mix_k': jnp.asarray(tmk), 'time_mix_v': jnp.asarray(tmv), 'time_mix_r': jnp.asarray(tmr), 'Wk': jax.random.normal(ks[1], (C, C), dtype=jnp.float32) * scale, 'Wv': jax.random.normal(ks[2], (C, C), dtype=jnp.float32) * scale, 'Wr': jax.random.normal(ks[3], (C, C), dtype=jnp.float32) * scale, 'Wo': jax.random.normal(ks[4], (C, C), dtype=jnp.float32) * scale}
    _L0_attn_all = _L0_attn_setup()
    _L0_attn_in = {k: v for k, v in _L0_attn_all.items() if k in ('time_decay', 'time_first', 'time_mix_k', 'time_mix_v', 'time_mix_r', 'Wk', 'Wv', 'Wr', 'Wo')}
    del _L0_attn_all

    def _L0_ffn_setup():
        import jax, jax.numpy as jnp
        import numpy as np
        B, S, D, H, E, K = (1, 512, 192, 384, 8, 2)
        key = jax.random.key(seed)
        ks = jax.random.split(key, 6)
        scale_d = 1.0 / np.sqrt(D)
        scale_h = 1.0 / np.sqrt(H)
        return {'x': jax.random.normal(ks[0], (B, S, D), dtype=jnp.float32), 'Wg': jax.random.uniform(ks[1], (D, E), minval=-scale_d, maxval=scale_d, dtype=jnp.float32), 'W1': jax.random.uniform(ks[2], (E, D, H), minval=-scale_d, maxval=scale_d, dtype=jnp.float32), 'b1': jax.random.uniform(ks[3], (E, H), minval=-scale_d, maxval=scale_d, dtype=jnp.float32), 'W2': jax.random.uniform(ks[4], (E, H, D), minval=-scale_h, maxval=scale_h, dtype=jnp.float32), 'b2': jax.random.uniform(ks[5], (E, D), minval=-scale_h, maxval=scale_h, dtype=jnp.float32)}
    _L0_ffn_all = _L0_ffn_setup()
    _L0_ffn_in = {k: v for k, v in _L0_ffn_all.items() if k in ('Wg', 'W1', 'b1', 'W2', 'b2')}
    del _L0_ffn_all
    return {'x': x, 'x_txt': x_txt, 'L0_tok_W': _L0_tok_in['W'], 'L0_tok_b': _L0_tok_in['b'], 'L0_txt_basin_coords': _L0_txt_in['basin_coords'], 'L0_txt_proj_w': _L0_txt_in['proj_w'], 'L0_txt_norm_w': _L0_txt_in['norm_w'], 'L0_attn_time_decay': _L0_attn_in['time_decay'], 'L0_attn_time_first': _L0_attn_in['time_first'], 'L0_attn_time_mix_k': _L0_attn_in['time_mix_k'], 'L0_attn_time_mix_v': _L0_attn_in['time_mix_v'], 'L0_attn_time_mix_r': _L0_attn_in['time_mix_r'], 'L0_attn_Wk': _L0_attn_in['Wk'], 'L0_attn_Wv': _L0_attn_in['Wv'], 'L0_attn_Wr': _L0_attn_in['Wr'], 'L0_attn_Wo': _L0_attn_in['Wo'], 'L0_ffn_Wg': _L0_ffn_in['Wg'], 'L0_ffn_W1': _L0_ffn_in['W1'], 'L0_ffn_b1': _L0_ffn_in['b1'], 'L0_ffn_W2': _L0_ffn_in['W2'], 'L0_ffn_b2': _L0_ffn_in['b2']}

def reference(x, x_txt, L0_tok_W, L0_tok_b, L0_txt_basin_coords, L0_txt_proj_w, L0_txt_norm_w, L0_attn_time_decay, L0_attn_time_first, L0_attn_time_mix_k, L0_attn_time_mix_v, L0_attn_time_mix_r, L0_attn_Wk, L0_attn_Wv, L0_attn_Wr, L0_attn_Wo, L0_ffn_Wg, L0_ffn_W1, L0_ffn_b1, L0_ffn_W2, L0_ffn_b2):
    import jax
    import jax.numpy as jnp

    def _L0_tok_ref(x, W, b):
        import jax, jax.numpy as jnp
        import numpy as np
        C_CURV = 1.0
        EPS = 1e-15
        BALL_EPS = 0.004

        def _artanh(x):
            x = jnp.clip(x, -1.0 + 1e-07, 1.0 - 1e-07)
            return jnp.arctanh(x)

        def _project(x):
            norm = jnp.maximum(jnp.linalg.norm(x, axis=-1, keepdims=True), EPS)
            maxnorm = (1.0 - BALL_EPS) / jnp.sqrt(C_CURV)
            return jnp.where(norm > maxnorm, x / norm * maxnorm, x)

        def _mobius_matvec(W, x):
            sqrt_c = jnp.sqrt(C_CURV)
            x_norm = jnp.maximum(jnp.linalg.norm(x, axis=-1, keepdims=True), EPS)
            mx = x @ W.T
            mx_norm = jnp.maximum(jnp.linalg.norm(mx, axis=-1, keepdims=True), EPS)
            res = jnp.tanh(mx_norm / x_norm * _artanh(sqrt_c * x_norm)) * mx / (mx_norm * sqrt_c)
            zero_row = jnp.all(mx == 0, axis=-1, keepdims=True)
            res = jnp.where(zero_row, jnp.zeros_like(res), res)
            return _project(res)

        def _mobius_add(x, y):
            c = C_CURV
            x2 = jnp.sum(x * x, axis=-1, keepdims=True)
            y2 = jnp.sum(y * y, axis=-1, keepdims=True)
            xy = jnp.sum(x * y, axis=-1, keepdims=True)
            num = (1.0 + 2.0 * c * xy + c * y2) * x + (1.0 - c * x2) * y
            denom = jnp.maximum(1.0 + 2.0 * c * xy + c * c * x2 * y2, EPS)
            return _project(num / denom)

        def _patchify(x, p):
            B, C, H, W = x.shape
            hp, wp = (H // p, W // p)
            x = x.reshape(B, C, hp, p, wp, p)
            x = x.transpose(0, 2, 4, 1, 3, 5)
            return x.reshape(B, hp * wp, C * p * p)
        p = 16
        B = x.shape[0]
        patches = _patchify(x, p)
        N, pd = (patches.shape[1], patches.shape[2])
        flat = patches.reshape(B * N, pd)
        out = _mobius_matvec(W, flat).reshape(B, N, W.shape[0])
        out = _mobius_add(out, b[None, None, :])
        return out

    def _L0_txt_ref(token_ids, basin_coords, proj_w, norm_w):
        import jax, jax.numpy as jnp
        import numpy as np
        import math
        VOCAB = 32000
        BASIN_DIM = 64
        D_MODEL = 192
        EPS = 1e-08
        basin = basin_coords[token_ids]
        emb = jnp.einsum('bsk,dk->bsd', basin, proj_w)
        x_f = emb.astype(jnp.float32)
        rms = jnp.sqrt(jnp.mean(x_f * x_f, axis=-1, keepdims=True) + EPS)
        y = (x_f / rms).astype(emb.dtype)
        return y * norm_w

    def _L0_attn_ref(x, time_decay, time_first, time_mix_k, time_mix_v, time_mix_r, Wk, Wv, Wr, Wo):
        import jax, jax.numpy as jnp
        import numpy as np
        import math
        N_LAYER, N_EMBD, LAYER_ID = (12, 192, 0)
        B, T, C = (32, 256, N_EMBD)

        def _init_params():
            r01 = LAYER_ID / (N_LAYER - 1)
            r1a0 = 1.0 - LAYER_ID / N_LAYER
            h = np.arange(C, dtype=np.float32)
            time_decay = (-5.0 + 8.0 * (h / (C - 1)) ** (0.7 + 1.3 * r01)).astype(np.float32)
            zigzag = np.array([(i + 1) % 3 - 1 for i in range(C)], dtype=np.float32) * 0.5
            time_first = (np.ones(C, dtype=np.float32) * math.log(0.3) + zigzag).astype(np.float32)
            xlin = (np.arange(C, dtype=np.float32) / C).reshape(1, 1, C)
            time_mix_k = np.power(xlin, r1a0).astype(np.float32)
            time_mix_v = (np.power(xlin, r1a0) + 0.3 * r01).astype(np.float32)
            time_mix_r = np.power(xlin, 0.5 * r1a0).astype(np.float32)
            return (time_decay, time_first, time_mix_k, time_mix_v, time_mix_r)

        def _wkv(w, u, k, v):

            def step(carry, kv):
                p, q, o = carry
                kt, vt = kv
                no = jnp.maximum(o, u + kt)
                A = jnp.exp(o - no)
                Bc = jnp.exp(u + kt - no)
                y = (A * p + Bc * vt) / (A * q + Bc)
                no2 = jnp.maximum(w + o, kt)
                A2 = jnp.exp(w + o - no2)
                B2 = jnp.exp(kt - no2)
                return ((A2 * p + B2 * vt, A2 * q + B2, no2), y)
            b = k.shape[0]
            init = (jnp.zeros((b, C), jnp.float32), jnp.zeros((b, C), jnp.float32), jnp.full((b, C), -1e+38, jnp.float32))
            kT = jnp.swapaxes(k, 0, 1)
            vT = jnp.swapaxes(v, 0, 1)
            _, ys = jax.lax.scan(step, init, (kT, vT))
            return jnp.swapaxes(ys, 0, 1)
        xx = jnp.pad(x, ((0, 0), (1, 0), (0, 0)))[:, :-1, :]
        xk = x * time_mix_k + xx * (1.0 - time_mix_k)
        xv = x * time_mix_v + xx * (1.0 - time_mix_v)
        xr = x * time_mix_r + xx * (1.0 - time_mix_r)
        k = jnp.einsum('btc,oc->bto', xk, Wk)
        v = jnp.einsum('btc,oc->bto', xv, Wv)
        r = jnp.einsum('btc,oc->bto', xr, Wr)
        sr = jax.nn.sigmoid(r)
        y = _wkv(time_decay, time_first, k, v)
        return jnp.einsum('btc,oc->bto', sr * y, Wo)

    def _L0_ffn_ref(x, Wg, W1, b1, W2, b2):
        import jax, jax.numpy as jnp
        import numpy as np
        B, S, D, H, E, K = (1, 512, 192, 384, 8, 2)
        gate_scores = jnp.einsum('bsd,de->bse', x, Wg)
        topk_scores, topk_idx = jax.lax.top_k(gate_scores, K)
        topk_probs = jax.nn.softmax(topk_scores, axis=-1)
        h = jax.nn.gelu(jnp.einsum('bsd,edh->bseh', x, W1) + b1, approximate=False)
        y = jnp.einsum('bseh,eho->bseo', h, W2) + b2
        y_sel = jnp.take_along_axis(y, topk_idx[..., None], axis=2)
        return jnp.sum(topk_probs[..., None] * y_sel, axis=2)
    h = _L0_tok_ref(x, L0_tok_W, L0_tok_b)
    h = jnp.concatenate([h, _L0_txt_ref(x_txt, L0_txt_basin_coords, L0_txt_proj_w, L0_txt_norm_w)], axis=1)
    h = h + _L0_attn_ref(_layernorm(h, axis=-1), L0_attn_time_decay, L0_attn_time_first, L0_attn_time_mix_k, L0_attn_time_mix_v, L0_attn_time_mix_r, L0_attn_Wk, L0_attn_Wv, L0_attn_Wr, L0_attn_Wo)
    h = h + _L0_ffn_ref(_layernorm(h, axis=-1), L0_ffn_Wg, L0_ffn_W1, L0_ffn_b1, L0_ffn_W2, L0_ffn_b2)
    return h

_drawn_inputs = setup_inputs


def setup_inputs(seed=0):
    import zlib

    import numpy as np

    out = dict(_drawn_inputs(seed))
    spreads = {'L0_txt_norm_w': (1.0, 0.2)}
    factors = {'L0_attn_time_first': 200.0,
     'L0_attn_time_mix_k': 8.0,
     'L0_attn_time_mix_r': 8.0,
     'L0_attn_Wk': 8.0,
     'L0_attn_Wr': 7.834,
     'L0_ffn_b1': 5.092}
    for name, (base, spread) in spreads.items():
        noise = np.random.default_rng([zlib.crc32(name.encode()), seed]).standard_normal(out[name].shape)
        drawn = base * np.exp(spread * noise) if base else spread * noise
        out[name] = jnp.asarray(drawn.astype(out[name].dtype))
    for name, factor in factors.items():
        out[name] = (out[name] * factor).astype(out[name].dtype)
    return out
```

```python
import concourse.bass as bass
from concourse import mybir
from contextlib import ExitStack

B, CH, HW, PATCH = 4, 3, 224, 16
D, PD, BASIN, VOCAB = 192, CH * PATCH * PATCH, 64, 32000
NP_, NT = (HW // PATCH) ** 2, 512
T = NP_ + NT
E, H = 8, 384
DA, DB = 128, D - 128
PAIR = 2
ROUNDS = B // PAIR
KP, KH, MOVE = PD // 128, H // 128, T // 2
TILES = [(0, NP_ // 2), (NP_ // 2, NP_ // 2)] + [(NP_ + 128 * j, 128) for j in range(NT // 128)]
NTILE = len(TILES)
NIMG = NP_ // 2
CHUNKS = [TILES[0:3], TILES[3:6]]
EPS, LN_EPS, RMS_EPS, MAXNORM = 1e-15, 1e-5, 1e-8, 1.0 - 0.004
ZMAX = 1.0 - 1e-7


def build(nc, xp, tokw, tokb, ids, basin, projt, normw, chan, attwa, attwb,
          w1a, w1b, b1t, w2, b2, wga, wgb, out):
    fp32, i32, u32 = mybir.dt.float32, mybir.dt.int32, mybir.dt.uint32
    ALU, ACT, AX = mybir.AluOpType, mybir.ActivationFunctionType, mybir.AxisListType
    ctx = ExitStack()
    with ctx:
        def sb(name, shape, dt=fp32):
            return ctx.enter_context(nc.sbuf_tensor(name, shape, dt))

        def sem(name):
            return ctx.enter_context(nc.semaphore(name))

        ident = sb("ident", [128, 128])
        ones = sb("ones", [128, 1])
        eiota = sb("eiota", [128, E])
        tokw_s = sb("tokw_s", [128, KP, D])
        tokb_s = sb("tokb_s", [128, D])
        normw_s = sb("normw_s", [128, D])
        projt_s = sb("projt_s", [BASIN, D])
        chan_s = sb("chan_s", [128, 5, 2])
        unmix = sb("unmix", [128, 5, 2])
        attwa_s = sb("attwa_s", [128, 4, D])
        attwb_s = sb("attwb_s", [128, 4, D])
        w1a_s = sb("w1a_s", [DA, E, H])
        w1b_s = sb("w1b_s", [DB, E, H])
        b1_s = sb("b1_s", [128, E, KH])
        w2_s = sb("w2_s", [128, E, KH, D])
        b2_s = sb("b2_s", [E, D])
        wga_s = sb("wga_s", [DA, E])
        wgb_s = sb("wgb_s", [DB, E])
        eps_s = sb("eps_s", [128, 2])
        bsq = sb("bsq", [128, 2])

        ids_s = sb("ids_s", [128, B * 4], i32)
        idf = sb("idf", [128, 2, B * 4])
        idc = sb("idc", [128, B * 4], u32)
        rows = sb("rows", [128, B * 4, BASIN])
        rowr = sb("rowr", [128, PAIR * 4, BASIN])
        xp_s = sb("xp_s", [128, KP, PAIR * NP_])
        mx = sb("mx", [NIMG, 4, D + 1])
        st = sb("st", [NIMG, 24, 4])
        ss = sb("ss", [128, PAIR * 4])
        rin = sb("rin", [128, PAIR * 4])
        scr = sb("scr", [128, D])
        scra = sb("scra", [128, D])
        carry, carryp = sb("carry", [1, 1]), sb("carryp", [1, 1])
        h = sb("h", [128, PAIR * NTILE, D])
        nrm = sb("nrm", [128, PAIR * NTILE, D])
        bn = sb("bn", [128, PAIR * NTILE, 6])
        mv = sb("mv", [128, PAIR * NTILE, 2])
        rstd = sb("rstd", [128, PAIR * NTILE])
        x3 = sb("x3", [128, 3, T + 1])
        xm = sb("xm", [128, 3, 3, T])
        zb = sb("zb", [128, 2, T])
        kvr = sb("kvr", [128, 3, 3, T])
        xsq = kvr[:].rearrange("p m l t -> p (m l t)")[:, 0:KP * PAIR * NP_].rearrange("p (k c) -> p k c", k=KP)
        osc = sb("osc", [128, T + 1])
        psc = sb("psc", [128, T + 1])
        qsc = sb("qsc", [128, T + 1])
        dif = sb("dif", [128, 4, T])
        ex = sb("ex", [128, 4, T])
        exf = ex[:].rearrange("p s t -> p (s t)")
        emb = exf[:, 0:PAIR * 4 * D].rearrange("p (j d) -> p j d", d=D)
        rowt = exf[0:BASIN, PAIR * 4 * D:PAIR * 4 * (D + 128)].rearrange("p (j n) -> p j n", n=128)
        bv = sb("bv", [128, T])
        num = sb("num", [128, T])
        nu2 = sb("nu2", [128, T])
        den = sb("den", [128, T])
        ys = kvr[:, 0]
        na, nb, gatet = xm[:, 0, 0:PAIR, :], xm[0:DB, 1, 0:PAIR, :], xm[0:E, 2, 0:PAIR, :]
        sc = sb("sc", [128, PAIR * NTILE, E])
        m8 = sb("m8", [128, PAIR * NTILE, 8])
        i8 = sb("i8", [128, PAIR * NTILE, 8], u32)
        ixf = sb("ixf", [128, PAIR * NTILE, 2])
        pr = sb("pr", [128, 4, PAIR * NTILE])
        oh = sb("oh", [128, 2, PAIR * NTILE, E])
        gate = sb("gate", [128, PAIR * NTILE, E])
        hid = dif[:].rearrange("p s t -> p (s t)")[:, 0:2 * KH * 384].rearrange("p (b j n) -> p b j n", b=2, j=KH)

        bank = [ctx.enter_context(nc.psum_tensor(f"bank{n}", [128, 512], fp32)) for n in range(8)]

        ids_in, emb_w_in, att_w_in, ffn_w_in = sem("ids_in"), sem("emb_w_in"), sem("att_w_in"), sem("ffn_w_in")
        xp_in, rows_in, out_done = sem("xp_in"), sem("rows_in"), sem("out_done")
        pool_c, vec_c, idc_ready = sem("pool_c"), sem("vec_c"), sem("idc_ready")
        vec = sem("vec")
        xsq_ready, img_mm, img_sb, img_S = sem("xsq_ready"), sem("img_mm"), sem("img_sb"), sem("img_S")
        a_act, a_vec = sem("a_act"), sem("a_vec")
        rowr_ready, rowt_mm, rowt_ready = sem("rowr_ready"), sem("rowt_mm"), sem("rowt_ready")
        emb_mm, emb_sb, ss_ready, rms_ready = sem("emb_mm"), sem("emb_sb"), sem("ss_ready"), sem("rms_ready")
        var_ready, std_ready, nrm_ready = sem("var_ready"), sem("std_ready"), sem("nrm_ready")
        tr_mm, tr_done = sem("tr_mm"), sem("tr_done")
        z_ready, z_used, xm_ready, kvr_mm, kvr_ready = (sem("z_ready"), sem("z_used"), sem("xm_ready"),
                                                        sem("kvr_mm"), sem("kvr_ready"))
        dif_ready, clip_ready, ex_ready, t2_ready, ys_ready = (sem("dif_ready"), sem("clip_ready"),
                                                               sem("ex_ready"), sem("t2_ready"), sem("ys_ready"))
        o_mm, o_added = sem("o_mm"), sem("o_added")
        gate_mm, gap_ready, e2_ready, gate_ready = sem("gate_mm"), sem("gap_ready"), sem("e2_ready"), sem("gate_ready")
        gt_mm, gt_ready, bias_mm, bias_added = sem("gt_mm"), sem("gt_ready"), sem("bias_mm"), sem("bias_added")
        up_mm, hid_ready, down_mm, y_added = sem("up_mm"), sem("hid_ready"), sem("down_mm"), sem("y_added")
        h_final = sem("h_final")

        IMG_T = [(b * NTILE + t, b * NP_ + t * NIMG) for b in range(PAIR) for t in range(2)]
        TXT_T = [b * NTILE + 2 + j for b in range(PAIR) for j in range(4)]
        ALL_T = [(b, t, *TILES[t]) for b in range(PAIR) for t in range(NTILE)]
        TRG = [(b, t0, t1, TILES[t0][0], sum(TILES[t][1] for t in range(t0, t1)))
               for b in range(PAIR) for t0, t1 in ((0, 4), (4, 6))]
        LN = 2
        NG = 2 * len(TRG)
        NKVR = 3 * 3 * 2
        STEPS = PAIR * len(CHUNKS) * E
        NALL = PAIR * NTILE
        VEC = 87

        block = ctx.enter_context(nc.Block())

        @block.sync
        def _(sp):
            sp.dma_start(ids_s[:], ids).then_inc(ids_in, 16)
            for dst, src in ((tokw_s, tokw), (tokb_s, tokb.partition_broadcast(128)),
                             (normw_s, normw.partition_broadcast(128)), (projt_s, projt)):
                sp.dma_start(dst[:], src).then_inc(emb_w_in, 16)
            for dst, src in ((chan_s, chan), (attwa_s, attwa), (attwb_s, attwb)):
                sp.dma_start(dst[:], src).then_inc(att_w_in, 16)
            for dst, src in ((w1a_s, w1a), (w1b_s, w1b), (b1_s, b1t), (w2_s, w2), (b2_s, b2), (wga_s, wga), (wgb_s, wgb)):
                sp.dma_start(dst[:], src).then_inc(ffn_w_in, 16)
            with sp.Fori(0, ROUNDS) as i:
                sp.wait_ge(h_final, i + 1)
                for b in range(PAIR):
                    for kind in (slice(0, 2), slice(2, NTILE)):
                        t0, p = TILES[kind][0]
                        n = len(TILES[kind])
                        dst = out[bass.ds(i * PAIR + b, 1), t0:t0 + n * p, :].rearrange("o (t p) d -> p (o t) d", p=p)
                        sp.dma_start(dst, h[0:p, b * NTILE + kind.start:b * NTILE + kind.stop, :]).then_inc(out_done, 16)
            sp.wait_ge(out_done, 16 + 16 * 2 * PAIR * ROUNDS)

        @block.gpsimd
        def _(pool):
            nc.gpsimd.memset(ones[:], 1.0).then_inc(pool_c, 1)
            nc.gpsimd.memset(ident[:], 0.0).then_inc(pool_c, 1)
            nc.gpsimd.iota(eiota[:], [[1, E]], base=0, channel_multiplier=0,
                           allow_small_or_imprecise_dtypes=True).then_inc(pool_c, 1)
            pool.wait_ge(pool_c, 3)
            nc.gpsimd.affine_select(out=ident[:], in_=ident[:], compare_op=ALU.not_equal, fill=1.0, base=0,
                                    pattern=[[-1, 128]], channel_multiplier=1).then_inc(pool_c, 1)
            pool.wait_ge(idc_ready, 1)
            for j in range(B * 4):
                nc.gpsimd.indirect_dma_start(
                    out=rows[:, j, :], out_offset=None, in_=basin,
                    in_offset=bass.IndirectOffsetOnAxis(ap=idc[:, j:j + 1], axis=0)).then_inc(rows_in, 16)
            with pool.Fori(0, ROUNDS) as i:
                for l in range(3):
                    g = i * 3 + l
                    pool.wait_ge(dif_ready, g + 1)
                    nc.gpsimd.tensor_tensor(carryp[:], ones[0:1, :], ones[0:1, :], op=ALU.mult)
                    for s in range(2):
                        nc.gpsimd.tensor_scalar(dif[:, 2 + s, :], dif[:, s, :], 3e38, 0.0, op0=ALU.min, op1=ALU.max)\
                            .then_inc(clip_ready, 1)
                    for s in range(2):
                        nc.gpsimd.tensor_scalar(dif[:, s, :], dif[:, s, :], 0.0, -3e38, op0=ALU.min, op1=ALU.max)\
                            .then_inc(clip_ready, 1)
                    pool.wait_ge(ex_ready, g * 4 + 4)
                    nc.gpsimd.tensor_tensor(nu2[:], ex[:, 3, :], kvr[:, 1, l, :], op=ALU.mult).then_inc(t2_ready, 1)

        @block.scalar
        def _(act):
            with act.Fori(0, ROUNDS) as i:
                act.wait_ge(img_mm, i * 4 + 1)
                act.dma_start(xp_s[:], xp[:, :, bass.ds(i * PAIR * NP_, PAIR * NP_)]).then_inc(xp_in, 16)
                act.wait_ge(xp_in, 16 * i + 16)
                nc.scalar.activation(xsq, xp_s[:], ACT.Square).then_inc(xsq_ready, 1)
                for q in range(4):
                    act.wait_ge(img_sb, i * 4 + q + 1)
                    if q:
                        act.wait_ge(img_S, i * 8 + q)
                    nc.scalar.activation(scra[0:NIMG, :], mx[:, q, 0:D], ACT.Square,
                                         accum_out=st[:, 1, q:q + 1]).then_inc(img_S, 1)
                act.wait_ge(img_S, i * 8 + 4)
                act.wait_ge(a_vec, i * 4 + 1)
                nc.scalar.activation(st[:, 2:4, :], st[:, 0:2, :], ACT.Sqrt).then_inc(a_act, 1)
                act.wait_ge(a_vec, i * 4 + 2)
                nc.scalar.activation(st[:, 8, :], st[:, 7, :], ACT.Ln).then_inc(a_act, 1)
                act.wait_ge(a_vec, i * 4 + 3)
                nc.scalar.activation(st[:, 10, :], st[:, 9, :], ACT.Tanh, scale=0.5).then_inc(a_act, 1)
                for q in range(4):
                    act.wait_ge(a_vec, i * 4 + 4)
                    if q:
                        act.wait_ge(img_S, i * 8 + 4 + q)
                    nc.scalar.activation(scra[0:NIMG, :], h[0:NIMG, IMG_T[q][0], :], ACT.Square,
                                         accum_out=st[:, 20, q:q + 1]).then_inc(img_S, 1)
                act.wait_ge(img_S, i * 8 + 8)
                nc.scalar.activation(st[:, 21, :], st[:, 20, :], ACT.Sqrt).then_inc(a_act, 1)
                for g in range(2):
                    act.wait_ge(rowt_mm, i * 2 + g + 1)
                    nc.scalar.activation(rowt[:, 4 * g:4 * g + 4, :], bank[2 + g][0:BASIN, :].rearrange(
                        "p (j n) -> p j n", j=4), ACT.Copy).then_inc(rowt_ready, 1)
                for j in range(PAIR * 4):
                    act.wait_ge(emb_sb, i * 4 + j // 2 + 1)
                    if j:
                        act.wait_ge(ss_ready, i * PAIR * 4 + j)
                    nc.scalar.activation(scra[:], emb[:, j, :], ACT.Square,
                                         accum_out=ss[:, j:j + 1]).then_inc(ss_ready, 1)
                act.wait_ge(ss_ready, (i + 1) * PAIR * 4)
                nc.scalar.activation(rin[:], ss[:], ACT.Sqrt, scale=1.0 / D, bias=eps_s[:, 1:2]).then_inc(rms_ready, 1)

                def layer_norm(n, dst):
                    act.wait_ge(var_ready, i * LN + n + 1)
                    nc.scalar.activation(rstd[:], mv[:, :, 1], ACT.Sqrt, bias=eps_s[:, 0:1]).then_inc(std_ready, 1)
                    for g in range(NG):
                        act.wait_ge(tr_mm, (i * LN + n) * NG + g + 1)
                        b, _, _, c0, cn = TRG[g // 2]
                        src = bank[g][0:DA if g % 2 == 0 else DB, 0:cn]
                        nc.scalar.activation(dst(b, g % 2, c0, cn), src, ACT.Copy).then_inc(tr_done, 1)

                layer_norm(0, lambda b, part, c0, cn:
                           x3[:, b, 1 + c0:1 + c0 + cn] if part == 0 else
                           x3[DB * b:DB * b + DB, 2, 1 + c0:1 + c0 + cn])
                act.wait_ge(tr_done, (i * LN + 1) * NG)
                act.wait_ge(att_w_in, 16 * 3)
                for m in range(3):
                    for l in range(3):
                        n = m * 3 + l
                        act.wait_ge(vec_c, 3)
                        if n >= 2:
                            act.wait_ge(xm_ready, i * 9 + n - 1)
                        nc.scalar.activation(zb[:, n % 2, :], x3[:, l, 0:T], ACT.Copy,
                                             scale=unmix[:, 2 + m, l // 2:l // 2 + 1]).then_inc(z_ready, 1)
                for n in range(NKVR):
                    m, l, half = n // 6, n // 2 % 3, n % 2
                    act.wait_ge(kvr_mm, i * NKVR + n + 1)
                    nc.scalar.activation(kvr[:, m, l, half * MOVE:half * MOVE + MOVE], bank[n % 8][:, 0:MOVE],
                                         ACT.Exp if m == 2 else ACT.Copy,
                                         scale=-1.0 if m == 2 else 1.0).then_inc(kvr_ready, 1)
                for l in range(3):
                    g = i * 3 + l
                    for s, (src, sign) in enumerate(((2, -1.0), (3, -1.0), (0, 1.0), (1, 1.0))):
                        act.wait_ge(clip_ready, g * 4 + s + 1)
                        nc.scalar.activation(ex[:, EXI[s], :], dif[:, src, :], ACT.Exp, scale=sign).then_inc(ex_ready, 1)
                layer_norm(1, lambda b, part, c0, cn: (na if part == 0 else nb)[:, b, c0:c0 + cn])
                act.wait_ge(gap_ready, i + 1)
                nc.scalar.activation(pr[:, 1, :], pr[:, 0, :], ACT.Exp).then_inc(e2_ready, 1)
                for g in range(len(TRG)):
                    act.wait_ge(gt_mm, i * len(TRG) + g + 1)
                    b, _, _, c0, cn = TRG[g]
                    nc.scalar.activation(gatet[:, b, c0:c0 + cn], bank[g][0:E, 0:cn], ACT.Copy).then_inc(gt_ready, 1)
                for s in range(STEPS):
                    e, tiles = s % E, CHUNKS[s // E % len(CHUNKS)]
                    cn = sum(p for _, p in tiles)
                    for j in range(KH):
                        n = s * KH + j
                        act.wait_ge(up_mm, i * STEPS * KH + n + 1)
                        if s >= 2:
                            act.wait_ge(down_mm, i * STEPS * 3 + (s - 1) * 3)
                        nc.scalar.activation(hid[:, s % 2, j, 0:cn], bank[n % 4][:, 0:cn], ACT.Gelu,
                                             bias=b1_s[:, e, j:j + 1]).then_inc(hid_ready, 1)

        @block.tensor
        def _(pe):
            pe.wait_ge(pool_c, 4)
            pe.wait_ge(emb_w_in, 16 * 4)
            with pe.Fori(0, ROUNDS) as i:
                pe.wait_ge(xp_in, 16 * i + 16)
                pe.wait_ge(xsq_ready, i + 1)
                for q in range(4):
                    if q >= 2:
                        pe.wait_ge(img_sb, i * 4 + q - 1)
                    if q == 3:
                        pe.wait_ge(rowr_ready, i + 1)
                    c0 = IMG_T[q][1]
                    for k in range(KP):
                        nc.tensor.matmul(bank[q % 2][0:NIMG, 0:D], xp_s[:, k, c0:c0 + NIMG], tokw_s[:, k, :],
                                         start=(k == 0), stop=(k == KP - 1))
                    for k in range(KP):
                        last = nc.tensor.matmul(bank[q % 2][0:NIMG, D:D + 1], xsq[:, k, c0:c0 + NIMG], ones[:],
                                                start=(k == 0), stop=(k == KP - 1))
                    last.then_inc(img_mm, 1)
                for g in range(2):
                    for j in range(4):
                        last = nc.tensor.transpose(bank[2 + g][0:BASIN, 128 * j:128 * j + 128],
                                                   rowr[:, 4 * g + j, :], ident[:])
                    last.then_inc(rowt_mm, 1)
                for j in range(PAIR * 4):
                    pe.wait_ge(rowt_ready, i * 2 + j // 4 + 1)
                    last = nc.tensor.matmul(bank[4 + j // 2][:, (j % 2) * D:(j % 2) * D + D], rowt[:, j, :],
                                            projt_s[:], start=True, stop=True)
                    if j % 2:
                        last.then_inc(emb_mm, 1)

                def transposes(n):
                    for g in range(NG):
                        b, t0, t1, c0, _ = TRG[g // 2]
                        f0, fn = (0, DA) if g % 2 == 0 else (DA, DB)
                        for t in range(t0, t1):
                            if g % 2 == 0:
                                pe.wait_ge(nrm_ready, (i * LN + n) * NALL + b * NTILE + t + 1)
                            off, p = TILES[t]
                            last = nc.tensor.transpose(bank[g][0:fn, off - c0:off - c0 + p],
                                                       nrm[0:p, b * NTILE + t, f0:f0 + fn], ident[0:p, 0:p])
                        last.then_inc(tr_mm, 1)

                transposes(0)
                pe.wait_ge(att_w_in, 16 * 3)
                for n in range(NKVR):
                    m, l, half = n // 6, n // 2 % 3, n % 2
                    pe.wait_ge(xm_ready, i * 9 + 3 * m + 3)
                    if n >= 8:
                        pe.wait_ge(kvr_ready, i * NKVR + n - 7)
                    cols = slice(half * MOVE, half * MOVE + MOVE)
                    outs = [(l, 0, DA, 0)] if l < 2 else [(b, DA, D, DB * b) for b in range(PAIR)]
                    for b, o0, o1, at in outs:
                        dst = bank[n % 8][at:at + o1 - o0, 0:MOVE]
                        nc.tensor.matmul(dst, attwa_s[:, m, o0:o1], xm[:, m, b, cols], start=True, stop=False)
                        last = nc.tensor.matmul(dst, attwb_s[DB * b:DB * b + DB, m, o0:o1],
                                                xm[DB * b:DB * b + DB, m, 2, cols], start=False, stop=True)
                    last.then_inc(kvr_mm, 1)
                for n, (b, t, off, p) in enumerate(ALL_T):
                    pe.wait_ge(ys_ready, i * 3 + 3)
                    if n >= 8:
                        pe.wait_ge(o_added, i * NALL + n - 7)
                    dst = bank[n % 8][0:p, 0:D]
                    nc.tensor.matmul(dst, ys[:, b, off:off + p], attwa_s[:, 3, :], start=True, stop=False)
                    nc.tensor.matmul(dst, ys[DB * b:DB * b + DB, 2, off:off + p], attwb_s[DB * b:DB * b + DB, 3, :],
                                     start=False, stop=True).then_inc(o_mm, 1)
                transposes(1)
                pe.wait_ge(tr_done, (i + 1) * LN * NG)
                pe.wait_ge(ffn_w_in, 16 * 7)
                for n, (b, t, off, p) in enumerate(ALL_T):
                    dst = bank[7][0:p, E * n:E * n + E]
                    nc.tensor.matmul(dst, na[:, b, off:off + p], wga_s[:], start=True, stop=False)
                    last = nc.tensor.matmul(dst, nb[:, b, off:off + p], wgb_s[:], start=False, stop=True)
                last.then_inc(gate_mm, 1)
                pe.wait_ge(gate_ready, i + 1)
                for g in range(len(TRG)):
                    b, t0, t1, c0, _ = TRG[g]
                    for t in range(t0, t1):
                        off, p = TILES[t]
                        last = nc.tensor.transpose(bank[g][0:E, off - c0:off - c0 + p],
                                                   gate[0:p, b * NTILE + t, :], ident[0:p, 0:p])
                    last.then_inc(gt_mm, 1)
                pe.wait_ge(gt_ready, (i + 1) * len(TRG))
                for n, (b, t, off, p) in enumerate(ALL_T):
                    if n >= 4:
                        pe.wait_ge(bias_added, i * NALL + n - 3)
                    nc.tensor.matmul(bank[4 + n % 4][0:p, 0:D], gatet[:, b, off:off + p], b2_s[:],
                                     start=True, stop=True).then_inc(bias_mm, 1)
                pe.wait_ge(bias_added, (i + 1) * NALL)

                def up(s):
                    b, c, e = s // (E * 2), s // E % 2, s % E
                    tiles = CHUNKS[c]
                    c0, cn = tiles[0][0], sum(p for _, p in tiles)
                    for j in range(KH):
                        n = s * KH + j
                        if n >= 4:
                            pe.wait_ge(hid_ready, i * STEPS * KH + n - 3)
                        dst = bank[n % 4][:, 0:cn]
                        nc.tensor.matmul(dst, w1a_s[:, e, 128 * j:128 * j + 128], na[:, b, c0:c0 + cn],
                                         start=True, stop=False)
                        nc.tensor.matmul(dst, w1b_s[:, e, 128 * j:128 * j + 128], nb[:, b, c0:c0 + cn],
                                         start=False, stop=True).then_inc(up_mm, 1)

                def down(s):
                    c, e = s // E % 2, s % E
                    pe.wait_ge(hid_ready, i * STEPS * KH + s * KH + KH)
                    c0 = CHUNKS[c][0][0]
                    for t, (off, p) in enumerate(CHUNKS[c]):
                        n = s * 3 + t
                        if n >= 4:
                            pe.wait_ge(y_added, i * STEPS * 3 + n - 3)
                        for j in range(KH):
                            last = nc.tensor.matmul(bank[4 + n % 4][0:p, 0:D], hid[:, s % 2, j, off - c0:off - c0 + p],
                                                    w2_s[:, e, j, :], start=(j == 0), stop=(j == KH - 1))
                        last.then_inc(down_mm, 1)

                for s in range(STEPS):
                    up(s)
                    if s:
                        down(s - 1)
                down(STEPS - 1)

        @block.vector
        def _(dve):
            V = nc.vector
            V.memset(x3[:, :, 0:1], 0.0)
            V.memset(osc[:, 0:1], -1e38).then_inc(img_mm, 1)
            V.memset(psc[:, 0:1], 0.0).then_inc(out_done, 16)
            V.memset(qsc[:, 0:1], 0.0)
            V.memset(sc[:], 0.0)
            V.memset(mv[:], 1.0)
            V.memset(eps_s[:, 0:1], LN_EPS)
            V.memset(eps_s[:, 1:2], RMS_EPS).then_inc(vec_c, 1)
            dve.wait_ge(ids_in, 16)
            V.tensor_scalar(idf[:, 0, :], ids_s[:], 0.0, float(VOCAB), op0=ALU.is_lt, op1=ALU.mult).then_inc(vec, 1)
            dve.wait_ge(vec, 1)
            V.tensor_tensor(idf[:, 1, :], ids_s[:], idf[:, 0, :], op=ALU.add).then_inc(vec, 1)
            dve.wait_ge(vec, 2)
            V.tensor_scalar(idc[:], idf[:, 1, :], 0.0, float(VOCAB - 1), op0=ALU.max, op1=ALU.min).then_inc(idc_ready, 1)
            dve.wait_ge(emb_w_in, 16 * 4)
            V.tensor_tensor_reduce(out=scr[:], in0=tokb_s[:], in1=tokb_s[:], scale=1.0, scalar=0.0,
                                   op0=ALU.mult, op1=ALU.add, accum_out=bsq[:, 0:1]).then_inc(vec, 1)
            dve.wait_ge(vec, 3)
            V.tensor_scalar_add(bsq[:, 1:2], bsq[:, 0:1], 1.0).then_inc(vec_c, 1)
            dve.wait_ge(att_w_in, 16 * 3)
            V.tensor_scalar(unmix[:], chan_s[:], -1.0, 1.0, op0=ALU.mult, op1=ALU.add).then_inc(vec_c, 1)
            dve.wait_ge(vec_c, 3)
            dve.wait_ge(pool_c, 4)
            PRE = 3
            with dve.Fori(0, ROUNDS) as i:
                steps = [0]

                def link(ins, alone=False):
                    steps[0] += 1
                    ins.then_inc(vec, 1)
                    dve.wait_ge(vec, i * VEC + PRE + steps[0])
                    if alone:
                        V.memset(carry[:], 0.0)

                dve.wait_ge(out_done, i * 16 * 2 * PAIR + 16)
                dve.wait_ge(rows_in, 16 * B * 4)
                V.tensor_copy(rowr[:], rows[:, bass.ds(i * PAIR * 4, PAIR * 4), :]).then_inc(rowr_ready, 1)
                b_img = tokb_s[0:NIMG, :]
                for q in range(4):
                    dve.wait_ge(img_mm, i * 4 + q + 2)
                    V.tensor_copy(mx[:, q, :], bank[q % 2][0:NIMG, 0:D + 1]).then_inc(img_sb, 1)
                    dve.wait_ge(img_sb, i * 4 + q + 1)
                    link(V.tensor_tensor_reduce(out=scr[0:NIMG, :], in0=mx[:, q, 0:D], in1=b_img, scale=1.0,
                                                scalar=0.0, op0=ALU.mult, op1=ALU.add, accum_out=st[:, 4, q:q + 1]))
                    V.tensor_reduce(st[:, 5, q:q + 1], mx[:, q, 0:D], axis=AX.X, op=ALU.max,
                                    apply_absolute_value=True)

                def row(n):
                    return st[:, n, :]

                V.tensor_copy(row(0), mx[:, :, D]).then_inc(a_vec, 1)
                dve.wait_ge(a_act, i * 4 + 1)
                link(V.tensor_scalar_max(st[:, 2:4, :], st[:, 2:4, :], EPS))
                link(V.tensor_scalar_min(row(6), row(2), ZMAX))
                link(V.tensor_scalar(row(7), row(6), -1.0, 1.0, op0=ALU.mult, op1=ALU.add))
                link(V.reciprocal(row(8), row(7)))
                link(V.scalar_tensor_tensor(row(6), row(6), 2.0, row(8), op0=ALU.mult, op1=ALU.mult))
                V.tensor_scalar_add(row(7), row(6), 1.0).then_inc(a_vec, 1)
                dve.wait_ge(a_vec, i * 4 + 2)
                link(V.tensor_scalar_add(row(11), row(7), -1.0))
                link(V.tensor_single_scalar(row(12), row(11), 0.0, op=ALU.is_equal))
                link(V.tensor_tensor(row(11), row(11), row(12), op=ALU.add))
                link(V.reciprocal(row(13), row(11)))
                dve.wait_ge(a_act, i * 4 + 2)
                link(V.tensor_tensor(row(8), row(8), row(12), op=ALU.add))
                link(V.tensor_tensor(row(8), row(8), row(6), op=ALU.mult))
                link(V.tensor_tensor(row(8), row(8), row(13), op=ALU.mult))
                link(V.reciprocal(row(14), row(2)))
                link(V.tensor_tensor(row(14), row(14), row(3), op=ALU.mult))
                V.tensor_tensor(row(9), row(14), row(8), op=ALU.mult).then_inc(a_vec, 1)
                link(V.reciprocal(row(15), row(3)))
                link(V.tensor_single_scalar(row(16), row(5), 0.0, op=ALU.is_gt))
                link(V.tensor_tensor(row(15), row(15), row(16), op=ALU.mult))
                dve.wait_ge(a_act, i * 4 + 3)
                link(V.tensor_tensor(row(15), row(15), row(10), op=ALU.mult))
                link(V.tensor_tensor(row(16), row(15), row(3), op=ALU.mult))
                link(V.tensor_scalar_max(row(16), row(16), EPS))
                link(V.reciprocal(row(17), row(16)))
                link(V.tensor_scalar(row(17), row(17), MAXNORM, 1.0, op0=ALU.mult, op1=ALU.min))
                link(V.tensor_tensor(row(15), row(15), row(17), op=ALU.mult))
                link(V.tensor_tensor(row(16), row(15), row(15), op=ALU.mult))
                link(V.tensor_tensor(row(16), row(16), row(1), op=ALU.mult))
                link(V.tensor_tensor(row(17), row(15), row(4), op=ALU.mult))
                link(V.tensor_scalar(row(18), row(17), 2.0, bsq[0:NIMG, 1:2], op0=ALU.mult, op1=ALU.add))
                link(V.tensor_scalar(row(17), row(17), 2.0, 1.0, op0=ALU.mult, op1=ALU.add))
                link(V.scalar_tensor_tensor(row(17), row(16), bsq[0:NIMG, 0:1], row(17), op0=ALU.mult, op1=ALU.add))
                link(V.tensor_scalar_max(row(17), row(17), EPS))
                link(V.reciprocal(row(19), row(17)))
                link(V.tensor_scalar(row(16), row(16), -1.0, 1.0, op0=ALU.mult, op1=ALU.add))
                link(V.tensor_tensor(row(16), row(16), row(19), op=ALU.mult))
                link(V.tensor_tensor(row(18), row(18), row(15), op=ALU.mult))
                link(V.tensor_tensor(row(18), row(18), row(19), op=ALU.mult))
                for q in range(4):
                    g = IMG_T[q][0]
                    link(V.tensor_scalar(h[0:NIMG, g, :], b_img, st[:, 16, q:q + 1], None, op0=ALU.mult))
                    last = V.scalar_tensor_tensor(h[0:NIMG, g, :], mx[:, q, 0:D], st[:, 18, q:q + 1],
                                                  h[0:NIMG, g, :], op0=ALU.mult, op1=ALU.add)
                last.then_inc(a_vec, 1)
                for g in range(4):
                    dve.wait_ge(emb_mm, i * 4 + g + 1)
                    V.tensor_copy(emb[:, 2 * g:2 * g + 2, :], bank[4 + g][:, 0:2 * D].rearrange(
                        "p (j d) -> p j d", j=2)).then_inc(emb_sb, 1)
                dve.wait_ge(a_act, i * 4 + 4)
                link(V.tensor_scalar_max(row(21), row(21), EPS))
                link(V.reciprocal(row(22), row(21)))
                link(V.tensor_scalar(row(22), row(22), MAXNORM, 1.0, op0=ALU.mult, op1=ALU.min))
                for q in range(4):
                    g = IMG_T[q][0]
                    V.tensor_scalar(h[0:NIMG, g, :], h[0:NIMG, g, :], st[:, 22, q:q + 1], None, op0=ALU.mult)
                dve.wait_ge(rms_ready, i + 1)
                link(V.reciprocal(rin[:], rin[:]))
                for j, g in enumerate(TXT_T):
                    last = V.scalar_tensor_tensor(h[:, g, :], emb[:, j, :], rin[:, j:j + 1], normw_s[:],
                                                  op0=ALU.mult, op1=ALU.mult)
                link(last)

                def layer_norm(n):
                    for g, (b, t, off, p) in enumerate(ALL_T):
                        last = V.bn_stats(bn[0:p, g, :], h[0:p, g, :])
                    link(last, alone=True)
                    for g, (b, t, off, p) in enumerate(ALL_T):
                        last = V.bn_aggr(mv[0:p, g, :], bn[0:p, g, :])
                    last.then_inc(var_ready, 1)
                    dve.wait_ge(std_ready, i * LN + n + 1)
                    link(V.reciprocal(rstd[:], rstd[:]))
                    for g, (b, t, off, p) in enumerate(ALL_T):
                        V.tensor_scalar(nrm[0:p, g, :], h[0:p, g, :], mv[0:p, g, 0:1], rstd[0:p, g:g + 1],
                                        op0=ALU.subtract, op1=ALU.mult).then_inc(nrm_ready, 1)

                layer_norm(0)
                dve.wait_ge(tr_done, (i * LN + 1) * NG)
                for m in range(3):
                    for l in range(3):
                        n = m * 3 + l
                        dve.wait_ge(z_ready, i * 9 + n + 1)
                        V.scalar_tensor_tensor(xm[:, m, l, :], x3[:, l, 1:T + 1], chan_s[:, 2 + m, l // 2:l // 2 + 1],
                                               zb[:, n % 2, :], op0=ALU.mult, op1=ALU.add).then_inc(xm_ready, 1)
                for l in range(3):
                    g = i * 3 + l
                    k, v, er = (kvr[:, m, l, :] for m in range(3))
                    w, u = chan_s[:, 0, l // 2:l // 2 + 1], chan_s[:, 1, l // 2:l // 2 + 1]
                    dve.wait_ge(kvr_ready, i * NKVR + 2 * l + 2)
                    link(V.tensor_tensor_scan(osc[:, 1:T + 1], w.to_broadcast([128, T]), k, -1e38,
                                              op0=ALU.add, op1=ALU.max))
                    V.scalar_tensor_tensor(dif[:, 0, :], osc[:, 0:T], w, k, op0=ALU.add, op1=ALU.subtract)
                    V.scalar_tensor_tensor(dif[:, 1, :], k, u, osc[:, 0:T], op0=ALU.add, op1=ALU.subtract)\
                        .then_inc(dif_ready, 1)
                    dve.wait_ge(kvr_ready, i * NKVR + 6 + 2 * l + 2)
                    dve.wait_ge(ex_ready, g * 4 + 1)
                    link(V.tensor_tensor(bv[:], ex[:, 0, :], v, op=ALU.mult))
                    dve.wait_ge(ex_ready, g * 4 + 3)
                    V.tensor_tensor_scan(psc[:, 1:T + 1], ex[:, 2, :], bv[:], 0.0, op0=ALU.mult, op1=ALU.add)
                    link(V.tensor_tensor_scan(qsc[:, 1:T + 1], ex[:, 2, :], ex[:, 0, :], 0.0, op0=ALU.mult, op1=ALU.add))
                    V.tensor_tensor(num[:], ex[:, 1, :], psc[:, 0:T], op=ALU.mult)
                    link(V.tensor_tensor(den[:], ex[:, 1, :], qsc[:, 0:T], op=ALU.mult))
                    dve.wait_ge(ex_ready, g * 4 + 4)
                    link(V.tensor_tensor(den[:], den[:], ex[:, 3, :], op=ALU.add))
                    dve.wait_ge(kvr_ready, i * NKVR + 12 + 2 * l + 2)
                    link(V.scalar_tensor_tensor(den[:], er, 1.0, den[:], op0=ALU.add, op1=ALU.mult))
                    dve.wait_ge(t2_ready, g + 1)
                    link(V.tensor_tensor(num[:], num[:], nu2[:], op=ALU.add))
                    link(V.reciprocal(den[:], den[:]))
                    V.tensor_tensor(ys[:, l, :], num[:], den[:], op=ALU.mult).then_inc(ys_ready, 1)
                for n, (b, t, off, p) in enumerate(ALL_T):
                    dve.wait_ge(o_mm, i * NALL + n + 1)
                    V.tensor_tensor(h[0:p, n, :], bank[n % 8][0:p, 0:D], h[0:p, n, :], op=ALU.add).then_inc(o_added, 1)
                dve.wait_ge(o_added, (i + 1) * NALL)
                layer_norm(1)
                dve.wait_ge(gate_mm, i + 1)
                for b in range(PAIR):
                    for p, t0, t1 in ((NIMG, 0, 2), (128, 2, NTILE)):
                        n0, n1 = b * NTILE + t0, b * NTILE + t1
                        last = V.tensor_copy(sc[0:p, n0:n1, :], bank[7][0:p, E * n0:E * n1].rearrange(
                            "p (n e) -> p n e", e=E))
                link(last, alone=True)
                for n in range(NALL):
                    last = V.max(m8[:, n, :], sc[:, n, :])
                link(last, alone=True)
                for n in range(NALL):
                    last = V.max_index(i8[:, n, :], m8[:, n, :], sc[:, n, :])
                V.tensor_tensor(pr[:, 0, :], m8[:, :, 1], m8[:, :, 0], op=ALU.subtract).then_inc(gap_ready, 1)
                link(last)
                link(V.tensor_copy(ixf[:], i8[:, :, 0:2]))
                both = [128, NALL, E]
                for s in range(2):
                    link(V.tensor_tensor(oh[:, s, :, :], ixf[:, :, s:s + 1].to_broadcast(both),
                                         eiota[:].rearrange("p (o e) -> p o e", o=1).to_broadcast(both), op=ALU.is_equal))
                dve.wait_ge(e2_ready, i + 1)
                link(V.tensor_scalar_add(pr[:, 2, :], pr[:, 1, :], 1.0))
                link(V.reciprocal(pr[:, 2, :], pr[:, 2, :]))
                link(V.tensor_tensor(pr[:, 3, :], pr[:, 1, :], pr[:, 2, :], op=ALU.mult))
                for s in range(2):
                    link(V.tensor_tensor(oh[:, s, :, :], oh[:, s, :, :],
                                         pr[:, 2 + s, :].rearrange("p (n o) -> p n o", o=1).to_broadcast(both), op=ALU.mult))
                V.tensor_tensor(gate[:], oh[:, 0, :, :], oh[:, 1, :, :], op=ALU.add).then_inc(gate_ready, 1)
                for n, (b, t, off, p) in enumerate(ALL_T):
                    dve.wait_ge(bias_mm, i * NALL + n + 1)
                    V.tensor_tensor(h[0:p, n, :], bank[4 + n % 4][0:p, 0:D], h[0:p, n, :], op=ALU.add)\
                        .then_inc(bias_added, 1)
                dve.wait_ge(bias_added, (i + 1) * NALL)
                for s in range(STEPS):
                    b, c, e = s // (E * 2), s // E % 2, s % E
                    for t, (off, p) in enumerate(CHUNKS[c]):
                        n = s * 3 + t
                        g = b * NTILE + 3 * c + t
                        dve.wait_ge(down_mm, i * STEPS * 3 + n + 1)
                        if e:
                            dve.wait_ge(y_added, i * STEPS * 3 + n - 2)
                        last = V.scalar_tensor_tensor(h[0:p, g, :], bank[4 + n % 4][0:p, 0:D], gate[0:p, g, e:e + 1],
                                                      h[0:p, g, :], op0=ALU.mult, op1=ALU.add)
                        last.then_inc(y_added, 1)
                dve.wait_ge(y_added, (i + 1) * STEPS * 3)
                V.tensor_copy(scr[0:1, 0:1], h[0:1, 0, 0:1]).then_inc(h_final, 1)
                assert steps[0] == VEC, steps[0]


EXI = (0, 1, 2, 3)
_INS = [("xp", (128, KP, B * NP_)), ("tokw", (128, KP, D)), ("tokb", (D,)), ("ids", (128, B * 4)),
        ("basin", (VOCAB, BASIN)), ("projt", (BASIN, D)), ("normw", (D,)), ("chan", (128, 5, 2)),
        ("attwa", (128, 4, D)), ("attwb", (128, 4, D)), ("w1a", (DA, E, H)), ("w1b", (DB, E, H)),
        ("b1t", (128, E, KH)), ("w2", (128, E, KH, D)), ("b2", (E, D)), ("wga", (DA, E)), ("wgb", (DB, E))]


def kernel(x, x_txt, L0_tok_W, L0_tok_b, L0_txt_basin_coords, L0_txt_proj_w, L0_txt_norm_w,
           L0_attn_time_decay, L0_attn_time_first, L0_attn_time_mix_k, L0_attn_time_mix_v, L0_attn_time_mix_r,
           L0_attn_Wk, L0_attn_Wv, L0_attn_Wr, L0_attn_Wo,
           L0_ffn_Wg, L0_ffn_W1, L0_ffn_b1, L0_ffn_W2, L0_ffn_b2):
    import numpy as np
    import concourse.bacc as bacc
    from concourse.bass_utils import run_bass_kernel_spmd

    side = HW // PATCH
    pix = np.asarray(x).reshape(B, CH, side, PATCH, side, PATCH).transpose(1, 3, 5, 0, 2, 4).reshape(KP, 128, B * NP_)
    chan = [np.asarray(a).reshape(D) for a in (L0_attn_time_decay, L0_attn_time_first, L0_attn_time_mix_k,
                                               L0_attn_time_mix_v, L0_attn_time_mix_r)]
    att = np.stack([np.asarray(a).T for a in (L0_attn_Wk, L0_attn_Wv, L0_attn_Wr, L0_attn_Wo)], axis=1)
    w1, w2, wg = np.asarray(L0_ffn_W1), np.asarray(L0_ffn_W2), np.asarray(L0_ffn_Wg)
    data = {
        "xp": pix.transpose(1, 0, 2),
        "tokw": np.asarray(L0_tok_W).T.reshape(KP, 128, D).transpose(1, 0, 2),
        "tokb": np.asarray(L0_tok_b),
        "ids": np.asarray(x_txt).reshape(B * 4, 128).T,
        "basin": np.asarray(L0_txt_basin_coords),
        "projt": np.asarray(L0_txt_proj_w).T,
        "normw": np.asarray(L0_txt_norm_w),
        "chan": np.stack([np.stack([a[:DA], np.concatenate([a[DA:], a[DA:]])], axis=1) for a in chan], axis=1),
        "attwa": att[:DA], "attwb": np.concatenate([att[DA:], att[DA:]]),
        "w1a": w1[:, :DA].transpose(1, 0, 2), "w1b": w1[:, DA:].transpose(1, 0, 2),
        "b1t": np.asarray(L0_ffn_b1).reshape(E, KH, 128).transpose(2, 0, 1),
        "w2": w2.reshape(E, KH, 128, D).transpose(2, 0, 1, 3),
        "b2": np.asarray(L0_ffn_b2),
        "wga": wg[:DA], "wgb": wg[DA:],
    }
    nc = bacc.Bacc("TRN2", target_bir_lowering=False, num_devices=1)
    arrays, args = {}, []
    for name, shape in _INS:
        a = np.ascontiguousarray(data[name])
        assert a.shape == shape, (name, a.shape)
        arrays[name] = a
        args.append(nc.dram_tensor(name, a.shape, mybir.dt.from_np(a.dtype), kind="ExternalInput").ap())
    args.append(nc.dram_tensor("out", (B, T, D), mybir.dt.float32, kind="ExternalOutput").ap())
    build(nc, *args)
    r = run_bass_kernel_spmd(nc, [arrays], core_ids=[0])
    return r.results[0]["out"]
```

```python
import concourse.bass as bass
from concourse import mybir
from contextlib import ExitStack

B, CH, HW, PATCH = 4, 3, 224, 16
D, PD, BASIN, VOCAB = 192, CH * PATCH * PATCH, 64, 32000
NP_, NT = (HW // PATCH) ** 2, 512
T = NP_ + NT
E, H = 8, 384
DA, DB = 128, D - 128
PAIR = 2
ROUNDS = B // PAIR
KP, KH, MOVE = PD // 128, H // 128, T // 2
TILES = [(0, NP_ // 2), (NP_ // 2, NP_ // 2)] + [(NP_ + 128 * j, 128) for j in range(NT // 128)]
NTILE = len(TILES)
NIMG = NP_ // 2
K = 2
EXP_TILES = -(-PAIR * T // 128)
SLOT_TILES = (K * PAIR * T + E * 127) // 128
SLOTS = SLOT_TILES * ROUNDS * 128
EPS, LN_EPS, RMS_EPS, MAXNORM = 1e-15, 1e-5, 1e-8, 1.0 - 0.004
ZMAX = 1.0 - 1e-7


def build(nc, xp, tokw, tokb, ids, basin, projt, normw, chan, attwa, attwb,
          w1a, w1b, w2, b2, wga, wgb, out, slot_x, slot_y):
    fp32, i32, u32 = mybir.dt.float32, mybir.dt.int32, mybir.dt.uint32
    ALU, ACT, AX = mybir.AluOpType, mybir.ActivationFunctionType, mybir.AxisListType
    ctx = ExitStack()
    with ctx:
        def sb(name, shape, dt=fp32):
            return ctx.enter_context(nc.sbuf_tensor(name, shape, dt))

        def sem(name):
            return ctx.enter_context(nc.semaphore(name))

        ident = sb("ident", [128, 128])
        ones = sb("ones", [128, 1])
        eiota = sb("eiota", [128, E])
        tokw_s = sb("tokw_s", [128, KP, D])
        tokb_s = sb("tokb_s", [128, D])
        normw_s = sb("normw_s", [128, D])
        projt_s = sb("projt_s", [BASIN, D])
        chan_s = sb("chan_s", [128, 5, 2])
        unmix = sb("unmix", [128, 5, 2])
        attwa_s = sb("attwa_s", [128, 4, D])
        attwb_s = sb("attwb_s", [128, 4, D])
        w1a_s = sb("w1a_s", [DA, E, H])
        w1b_s = sb("w1b_s", [DB + 1, E, H])
        w2_s = sb("w2_s", [128, E, KH, D])
        b2_s = sb("b2_s", [E, D])
        wga_s = sb("wga_s", [DA, E])
        wgb_s = sb("wgb_s", [DB, E])
        eps_s = sb("eps_s", [128, 2])
        bsq = sb("bsq", [128, 2])

        ids_s = sb("ids_s", [128, B * 4], i32)
        idf = sb("idf", [128, 2, B * 4])
        idc = sb("idc", [128, B * 4], u32)
        rows = sb("rows", [128, B * 4, BASIN])
        rowr = sb("rowr", [128, PAIR * 4, BASIN])
        mx = sb("mx", [NIMG, 4, D + 1])
        st = sb("st", [NIMG, 24, 4])
        ss = sb("ss", [128, PAIR * 4])
        rin = sb("rin", [128, PAIR * 4])
        carry, carryp = sb("carry", [1, 1]), sb("carryp", [1, 2])
        h = sb("h", [128, B * NTILE, D])
        nrm2 = sb("nrm2", [128, PAIR * NTILE, D])
        bn = sb("bn", [128, PAIR * NTILE, 6])
        mv = sb("mv", [128, PAIR * NTILE, 2])
        rstd = sb("rstd", [128, PAIR * NTILE])
        x3 = sb("x3", [128, 3, T + 1])
        xm = sb("xm", [128, 3, 3, T])
        zb = sb("zb", [128, 2, T])
        kvr = sb("kvr", [128, 3, 3, T])
        kvrf = kvr[:].rearrange("p m l t -> p (m l t)")
        NPX = KP * PAIR * NP_
        xsq, xp_s = (kvrf[:, n * NPX:(n + 1) * NPX].rearrange("p (k c) -> p k c", k=KP) for n in range(2))
        osc = sb("osc", [128, T + 1])
        psc = sb("psc", [128, T + 1])
        qsc = sb("qsc", [128, T + 1])
        dif = sb("dif", [128, 4, T])
        ex = sb("ex", [128, 4, T])
        exf = ex[:].rearrange("p s t -> p (s t)")
        emb = exf[:, 0:PAIR * 4 * D].rearrange("p (j d) -> p j d", d=D)
        rowt = exf[0:BASIN, PAIR * 4 * D:PAIR * 4 * (D + 128)].rearrange("p (j n) -> p j n", n=128)
        nrm = exf[:, 0:PAIR * NTILE * D].rearrange("p (n d) -> p n d", d=D)
        exl = [[ex[:, s, :] for s in range(4)],
               [xm[:, 0, 0, :], xm[:, 0, 1, :], xm[:, 0, 2, :], zb[:, 0, :]]]
        bv = sb("bv", [128, T])
        num = sb("num", [128, T])
        scr, scra = num[:, 0:D], num[:, D:2 * D]
        nu2_s = sb("nu2_s", [128, T])
        nu2 = [nu2_s[:], zb[:, 1, :]]
        den = sb("den", [128, T])
        ys = kvr[:, 0]
        na, nb, gatet = xm[:, 0, 0:PAIR, :], xm[0:DB, 1, 0:PAIR, :], xm[0:E, 2, 0:PAIR, :]
        sc = sb("sc", [128, PAIR * NTILE, E])
        m8 = sb("m8", [128, PAIR * NTILE, 8])
        i8 = sb("i8", [128, PAIR * NTILE, 8], u32)
        ixf = sb("ixf", [128, PAIR * NTILE, 2])
        pr = sb("pr", [128, 4, PAIR * NTILE])
        oh = sb("oh", [128, K, E, PAIR * NTILE])
        ohw = sb("ohw", [128, K, E, PAIR * NTILE])
        gate = sb("gate", [128, PAIR * NTILE, E])
        vmask = sb("vmask", [128, PAIR * NTILE])
        before = sb("before", [128, 128])
        all1 = sb("all1", [128, 128])
        thr = sb("thr", [128, EXP_TILES])
        siota = sb("siota", [1, SLOT_TILES])
        rmask = sb("rmask", [128, E, PAIR * NTILE])
        cnt = sb("cnt", [128, 4, E, PAIR * NTILE])
        per_e = sb("per_e", [128, 5, E])
        over = sb("over", [128, E, EXP_TILES])
        le = cnt[0:1].rearrange("p a e n -> p (a e n)")[:, 0:SLOT_TILES * E].rearrange("p (s e) -> p s e", e=E)
        emf = sb("emf", [1, SLOT_TILES])
        slot0 = sb("slot0", [128, 1])
        posf = sb("posf", [128, K, PAIR * NTILE])
        emap = sb("emap", [1, ROUNDS * SLOT_TILES], i32)
        pos = sb("pos", [128, K * PAIR * NTILE], u32)
        pos_all = sb("pos_all", [128, ROUNDS, K * PAIR * NTILE], u32)
        prob_all = sb("prob_all", [128, ROUNDS, K, PAIR * NTILE])
        posg = sb("posg", [128, ROUNDS, K * PAIR * NTILE], u32)
        diff = dif[:].rearrange("p s t -> p (s t)")

        def pair_of(start, width):
            return [diff[:, start + n * width:start + (n + 1) * width] for n in range(2)]

        xin, hid, xta, xtb, hidt, yo = (pair_of(a, w) for a, w in
                                        ((0, D), (384, H), (1152, 128), (1408, 128), (1664, H), (2432, D)))
        NYG = K * PAIR * NTILE
        yg = [f[:, 0:NYG * D].rearrange("p (n d) -> p n d", d=D)
              for f in (xm[:].rearrange("p m l t -> p (m l t)"), kvrf)]
        NZ = SLOT_TILES * ROUNDS // 4
        zeros = xm[:].rearrange("p m l t -> p (m l t)")[:, 0:NZ * D]

        bank = [ctx.enter_context(nc.psum_tensor(f"bank{n}", [128, 512], fp32)) for n in range(8)]

        ids_in, emb_w_in, att_w_in, ffn_w_in = sem("ids_in"), sem("emb_w_in"), sem("att_w_in"), sem("ffn_w_in")
        xp_in, rows_in, out_done = sem("xp_in"), sem("rows_in"), sem("out_done")
        pool_c, vec_c, idc_ready = sem("pool_c"), sem("vec_c"), sem("idc_ready")
        vec = sem("vec")
        xsq_ready, img_mm, img_sb, img_S = sem("xsq_ready"), sem("img_mm"), sem("img_sb"), sem("img_S")
        a_act, a_vec = sem("a_act"), sem("a_vec")
        rowr_ready, rowt_mm, rowt_ready = sem("rowr_ready"), sem("rowt_mm"), sem("rowt_ready")
        emb_mm, emb_sb, ss_ready, rms_ready = sem("emb_mm"), sem("emb_sb"), sem("ss_ready"), sem("rms_ready")
        var_ready, std_ready, nrm_ready = sem("var_ready"), sem("std_ready"), sem("nrm_ready")
        tr_mm, tr_done = sem("tr_mm"), sem("tr_done")
        z_ready, z_used, xm_ready, kvr_mm, kvr_ready = (sem("z_ready"), sem("z_used"), sem("xm_ready"),
                                                        sem("kvr_mm"), sem("kvr_ready"))
        dif_ready, relu_ready, ex_ready, t2_ready, ys_ready = (sem("dif_ready"), sem("relu_ready"),
                                                               sem("ex_ready"), sem("t2_ready"), sem("ys_ready"))
        o_mm, o_added = sem("o_mm"), sem("o_added")
        gate_mm, gap_ready, e2_ready, gate_ready = sem("gate_mm"), sem("gap_ready"), sem("e2_ready"), sem("gate_ready")
        gt_mm, gt_ready, bias_mm, bias_added = sem("gt_mm"), sem("gt_ready"), sem("bias_mm"), sem("bias_added")
        zeros_set, zeros_in, mask_ready, rank_mm = sem("zeros_set"), sem("zeros_in"), sem("mask_ready"), sem("rank_mm")
        pos_ready, scattered, emap_ready = sem("pos_ready"), sem("scattered"), sem("emap_ready")
        x_in = [sem("x_in0"), sem("x_in1")]
        y_out = [sem("y_out0"), sem("y_out1")]
        xt_mm, xt_ready, up_mm, hid_ready = sem("xt_mm"), sem("xt_ready"), sem("up_mm"), sem("hid_ready")
        ht_mm, ht_ready, down_mm, yo_ready = sem("ht_mm"), sem("ht_ready"), sem("down_mm"), sem("yo_ready")
        y_added = sem("y_added")
        posg_ready, gathered, h_final = sem("posg_ready"), [sem("gathered0"), sem("gathered1")], sem("h_final")

        IMG_T = [(b * NTILE + t, b * NP_ + t * NIMG) for b in range(PAIR) for t in range(2)]
        TXT_T = [b * NTILE + 2 + j for b in range(PAIR) for j in range(4)]
        ALL_T = [(b, t, *TILES[t]) for b in range(PAIR) for t in range(NTILE)]
        TRG = [(b, t0, t1, TILES[t0][0], sum(TILES[t][1] for t in range(t0, t1)))
               for b in range(PAIR) for t0, t1 in ((0, 4), (4, 6))]
        LN = 2
        NG = 2 * len(TRG)
        KVR = [(0, 0), (0, 1), (1, 0), (2, 0), (0, 2), (1, 1), (2, 1), (1, 2), (2, 2)]
        NKVR = len(KVR) * 2
        NSLOT = ROUNDS * SLOT_TILES
        NALL = PAIR * NTILE
        UNROLL = 6
        assert (NSLOT - 6) % UNROLL == 0 and UNROLL % 2 == 0
        VEC = 107

        block = ctx.enter_context(nc.Block())

        def hr(i, g, p):
            return h[0:p, bass.ds(i * NALL + g, 1), :].rearrange("p o d -> p (o d)")

        def cleared(n):
            return slot_x[n * NZ * 128:(n + 1) * NZ * 128, :].rearrange("(p j) d -> p (j d)", p=128)

        @block.sync
        def _(sp):
            sp.dma_start(ids_s[:], ids).then_inc(ids_in, 16)
            for dst, src in ((tokw_s, tokw), (tokb_s, tokb.partition_broadcast(128)),
                             (normw_s, normw.partition_broadcast(128)), (projt_s, projt)):
                sp.dma_start(dst[:], src).then_inc(emb_w_in, 16)
            for dst, src in ((chan_s, chan), (attwa_s, attwa), (attwb_s, attwb)):
                sp.dma_start(dst[:], src).then_inc(att_w_in, 16)
            sp.wait_ge(rows_in, 16 * PAIR * 4)
            for dst, src in ((w1a_s, w1a), (w1b_s, w1b), (w2_s, w2), (b2_s, b2), (wga_s, wga), (wgb_s, wgb)):
                sp.dma_start(dst[:], src).then_inc(ffn_w_in, 16)
            sp.wait_ge(zeros_set, 1)
            for n in range(3):
                sp.dma_start(cleared(n), zeros).then_inc(zeros_in, 16)

            def load(s, par):
                sp.dma_start(xin[par], slot_x[bass.ds(s * 128, 128), :]).then_inc(x_in[par], 16)

            def store(s, par):
                sp.wait_ge(yo_ready, s + 1)
                sp.dma_start(slot_y[bass.ds(s * 128, 128), :], yo[par]).then_inc(y_out[par], 16)

            for i in range(1, ROUNDS):
                sp.wait_ge(ys_ready, i * 3)
                sp.dma_start(xp_s, xp[:, :, i * PAIR * NP_:(i + 1) * PAIR * NP_]).then_inc(xp_in, 16)

            sp.wait_ge(scattered, 16 + 16 * NYG)
            sp.wait_ge(ys_ready, ROUNDS * 3)
            load(0, 0)
            load(1, 1)
            for s in range(2):
                sp.wait_ge(xt_mm, s + 1)
                load(s + 2, s)

            def rows_and_answers(lo, hi):
                with sp.Fori(lo // 2, hi // 2) as q:
                    for par in range(2):
                        s = q * 2 + par
                        sp.wait_ge(xt_mm, s - 1)
                        load(s, par)
                        store(s - 4, par)

            rows_and_answers(4, SLOT_TILES)
            sp.wait_ge(scattered, 16 + 16 * NYG * ROUNDS)
            rows_and_answers(SLOT_TILES, NSLOT)
            for s in range(NSLOT - 4, NSLOT):
                store(s, s % 2)
            with sp.Fori(0, ROUNDS) as i:
                sp.wait_ge(h_final, i + 1)
                for b in range(PAIR):
                    for kind in (slice(0, 2), slice(2, NTILE)):
                        t0, p = TILES[kind][0]
                        n = len(TILES[kind])
                        dst = out[bass.ds(i * PAIR + b, 1), t0:t0 + n * p, :].rearrange("o (t p) d -> p (o t) d", p=p)
                        sp.dma_start(dst, h[0:p, bass.ds(i * NALL + b * NTILE + kind.start, n), :]).then_inc(out_done, 16)
            sp.wait_ge(out_done, 16 * 2 * PAIR * ROUNDS)

        @block.gpsimd
        def _(pool):
            nc.gpsimd.memset(ones[:], 1.0).then_inc(pool_c, 1)
            nc.gpsimd.memset(ident[:], 0.0).then_inc(pool_c, 1)
            nc.gpsimd.iota(eiota[:], [[1, E]], base=0, channel_multiplier=0,
                           allow_small_or_imprecise_dtypes=True).then_inc(pool_c, 1)
            pool.wait_ge(pool_c, 3)
            nc.gpsimd.affine_select(out=ident[:], in_=ident[:], compare_op=ALU.not_equal, fill=1.0, base=0,
                                    pattern=[[-1, 128]], channel_multiplier=1).then_inc(pool_c, 1)

            def table_rows(i):
                for j in range(i * PAIR * 4, (i + 1) * PAIR * 4):
                    nc.gpsimd.indirect_dma_start(
                        out=rows[:, j, :], out_offset=None, in_=basin,
                        in_offset=bass.IndirectOffsetOnAxis(ap=idc[:, j:j + 1], axis=0)).then_inc(rows_in, 16)

            pool.wait_ge(idc_ready, 1)
            table_rows(0)
            nc.gpsimd.memset(zeros, 0.0).then_inc(zeros_set, 1)
            pool.wait_ge(rows_in, 16 * PAIR * 4)
            for i in range(1, ROUNDS):
                table_rows(i)
            pool.wait_ge(zeros_set, 1)
            pool.dma_start(cleared(3), zeros).then_inc(scattered, 16)
            nc.gpsimd.memset(all1[:], 1.0).then_inc(pool_c, 1)
            nc.gpsimd.memset(vmask[:], 1.0).then_inc(pool_c, 1)
            nc.gpsimd.iota(thr[:], [[128, EXP_TILES]], base=0, channel_multiplier=0,
                           allow_small_or_imprecise_dtypes=True).then_inc(pool_c, 1)
            nc.gpsimd.iota(siota[:], [[1, SLOT_TILES]], base=0, channel_multiplier=0,
                           allow_small_or_imprecise_dtypes=True).then_inc(pool_c, 1)
            pool.wait_ge(pool_c, 8)
            nc.gpsimd.affine_select(out=before[:], in_=all1[:], compare_op=ALU.is_gt, fill=0.0, base=0,
                                    pattern=[[1, 128]], channel_multiplier=-1).then_inc(pool_c, 1)
            for b in range(PAIR):
                cols = vmask[:, b * NTILE:b * NTILE + 2]
                nc.gpsimd.affine_select(out=cols, in_=cols, compare_op=ALU.is_gt, fill=0.0, base=NIMG,
                                        pattern=[[0, 2]], channel_multiplier=-1).then_inc(pool_c, 1)
            with pool.Fori(0, ROUNDS) as i:
                for l in range(3):
                    g = i * 3 + l
                    pool.wait_ge(kvr_ready, i * NKVR + 2 * KVR.index((1, l)) + 2)
                    pool.wait_ge(ex_ready, g * 4 + 4)
                    nc.gpsimd.tensor_tensor(nu2[l % 2], exl[l % 2][3], kvr[:, 1, l, :], op=ALU.mult).then_inc(t2_ready, 1)
                pool.wait_ge(zeros_in, 16 * 3)
                pool.wait_ge(scattered, 16)
                pool.wait_ge(pos_ready, i + 1)
                nc.gpsimd.tensor_tensor(carryp[:, 1:2], ones[0:1, :], ones[0:1, :], op=ALU.mult)
                for n, (b, t, off, p) in enumerate(ALL_T):
                    for k in range(K):
                        c = k * NALL + n
                        nc.gpsimd.indirect_dma_start(
                            out=slot_x, out_offset=bass.IndirectOffsetOnAxis(ap=pos[0:p, c:c + 1], axis=0),
                            in_=nrm2[0:p, n, :], in_offset=None).then_inc(scattered, 16)
            for i in range(ROUNDS):
                pool.wait_ge(posg_ready, 1)
                for par in range(2):
                    pool.wait_ge(y_out[par], 16 * SLOT_TILES // 2 * (i + 1))
                for n, (b, t, off, p) in enumerate(ALL_T):
                    for k in range(K):
                        c = k * NALL + n
                        nc.gpsimd.indirect_dma_start(
                            out=yg[i][0:p, c, :], out_offset=None, in_=slot_y[0:(i + 1) * SLOT_TILES * 128, :],
                            in_offset=bass.IndirectOffsetOnAxis(ap=posg[0:p, i, c:c + 1], axis=0))\
                            .then_inc(gathered[i], 16)

        @block.scalar
        def _(act):
            act.dma_start(xp_s, xp[:, :, 0:PAIR * NP_]).then_inc(xp_in, 16)
            with act.Fori(0, ROUNDS) as i:
                act.wait_ge(xp_in, 16 * i + 16)
                act.wait_ge(o_mm, i * NALL + 1)
                nc.scalar.activation(xsq, xp_s[:], ACT.Square).then_inc(xsq_ready, 1)
                for q in range(4):
                    act.wait_ge(img_sb, i * 4 + q + 1)
                    if q:
                        act.wait_ge(img_S, i * 8 + q)
                    nc.scalar.activation(scra[0:NIMG, :], mx[:, q, 0:D], ACT.Square,
                                         accum_out=st[:, 1, q:q + 1]).then_inc(img_S, 1)
                act.wait_ge(img_S, i * 8 + 4)
                act.wait_ge(a_vec, i * 4 + 1)
                nc.scalar.activation(st[:, 2:4, :], st[:, 0:2, :], ACT.Sqrt).then_inc(a_act, 1)
                for g in range(2):
                    act.wait_ge(rowt_mm, i * 2 + g + 1)
                    nc.scalar.activation(rowt[:, 4 * g:4 * g + 4, :], bank[2 + g][0:BASIN, :].rearrange(
                        "p (j n) -> p j n", j=4), ACT.Copy).then_inc(rowt_ready, 1)
                act.wait_ge(a_vec, i * 4 + 2)
                nc.scalar.activation(st[:, 8, :], st[:, 7, :], ACT.Ln).then_inc(a_act, 1)
                act.wait_ge(a_vec, i * 4 + 3)
                nc.scalar.activation(st[:, 10, :], st[:, 9, :], ACT.Tanh, scale=0.5).then_inc(a_act, 1)
                for j in range(PAIR * 4):
                    act.wait_ge(emb_sb, i * 4 + j // 2 + 1)
                    if j:
                        act.wait_ge(ss_ready, i * PAIR * 4 + j)
                    nc.scalar.activation(scra, emb[:, j, :], ACT.Square,
                                         accum_out=ss[:, j:j + 1]).then_inc(ss_ready, 1)
                for q in range(4):
                    act.wait_ge(a_vec, i * 4 + 4)
                    if q:
                        act.wait_ge(img_S, i * 8 + 4 + q)
                    else:
                        act.wait_ge(ss_ready, (i + 1) * PAIR * 4)
                    nc.scalar.activation(scra[0:NIMG, :], hr(i, IMG_T[q][0], NIMG), ACT.Square,
                                         accum_out=st[:, 20, q:q + 1]).then_inc(img_S, 1)
                act.wait_ge(img_S, i * 8 + 8)
                nc.scalar.activation(st[:, 21, :], st[:, 20, :], ACT.Sqrt).then_inc(a_act, 1)
                act.wait_ge(ss_ready, (i + 1) * PAIR * 4)
                nc.scalar.activation(rin[:], ss[:], ACT.Sqrt, scale=1.0 / D, bias=eps_s[:, 1:2]).then_inc(rms_ready, 1)

                def layer_norm(n, dst):
                    act.wait_ge(var_ready, i * LN + n + 1)
                    nc.scalar.activation(rstd[:], mv[:, :, 1], ACT.Sqrt, bias=eps_s[:, 0:1]).then_inc(std_ready, 1)
                    for g in range(NG):
                        act.wait_ge(tr_mm, (i * LN + n) * NG + g + 1)
                        b, _, _, c0, cn = TRG[g // 2]
                        src = bank[g][0:DA if g % 2 == 0 else DB, 0:cn]
                        nc.scalar.activation(dst(b, g % 2, c0, cn), src, ACT.Copy).then_inc(tr_done, 1)

                layer_norm(0, lambda b, part, c0, cn:
                           x3[:, b, 1 + c0:1 + c0 + cn] if part == 0 else
                           x3[DB * b:DB * b + DB, 2, 1 + c0:1 + c0 + cn])
                act.wait_ge(tr_done, (i * LN + 1) * NG)
                act.wait_ge(att_w_in, 16 * 3)
                for m in range(3):
                    for l in range(3):
                        n = m * 3 + l
                        act.wait_ge(vec_c, 3)
                        if n >= 2:
                            act.wait_ge(xm_ready, i * 9 + n - 1)
                        nc.scalar.activation(zb[:, n % 2, :], x3[:, l, 0:T], ACT.Copy,
                                             scale=unmix[:, 2 + m, l // 2:l // 2 + 1]).then_inc(z_ready, 1)
                def evacuate(first, last):
                    for n in range(2 * first, 2 * last):
                        m, l = KVR[n // 2]
                        half = n % 2 * MOVE
                        act.wait_ge(kvr_mm, i * NKVR + n + 1)
                        nc.scalar.activation(kvr[:, m, l, half:half + MOVE], bank[n % 8][:, 0:MOVE],
                                             ACT.Exp if m == 2 else ACT.Copy,
                                             scale=-1.0 if m == 2 else 1.0).then_inc(kvr_ready, 1)

                def exponentials(l):
                    g = i * 3 + l
                    for s, sign in ((0, 1.0), (2, -1.0), (1, 1.0), (3, -1.0)):
                        dst = exl[l % 2][s]
                        if (l, s) == (0, 0):
                            act.wait_ge(dif_ready, g + 1)
                        elif s == 0:
                            act.wait_ge(dif_ready, g + 1)
                            if l == 2:
                                act.wait_ge(ys_ready, g - 1)
                        n = g * 4 + (0, 2, 1, 3).index(s)
                        nc.scalar.activation(dst, dif[:, 2 * (l % 2) + s % 2, :], ACT.Relu, scale=sign)\
                            .then_inc(relu_ready, 1)
                        act.wait_ge(relu_ready, n + 1)
                        nc.scalar.activation(dst, dst, ACT.Exp, scale=-1.0).then_inc(ex_ready, 1)

                evacuate(0, 2)
                exponentials(0)
                evacuate(2, 5)
                exponentials(1)
                evacuate(5, 9)
                exponentials(2)
                layer_norm(1, lambda b, part, c0, cn: (na if part == 0 else nb)[:, b, c0:c0 + cn])
                act.wait_ge(gap_ready, i + 1)
                nc.scalar.activation(pr[:, 1, :], pr[:, 0, :], ACT.Exp).then_inc(e2_ready, 1)
                for g in range(len(TRG)):
                    act.wait_ge(gt_mm, i * len(TRG) + g + 1)
                    b, _, _, c0, cn = TRG[g]
                    nc.scalar.activation(gatet[:, b, c0:c0 + cn], bank[g][0:E, 0:cn], ACT.Copy).then_inc(gt_ready, 1)
            def gelu(s, par, first=False):
                act.wait_ge(up_mm, s + 1)
                if not first:
                    act.wait_ge(ht_mm, s - 1)
                nc.scalar.activation(hid[par], bank[2 + par][:, 0:H], ACT.Gelu).then_inc(hid_ready, 1)

            def answer(s, par, first=False):
                act.wait_ge(down_mm, s + 1)
                if not first:
                    act.wait_ge(y_out[par], y_stored(s, par))
                nc.scalar.activation(yo[par], bank[6 + par][:, 0:D], ACT.Copy).then_inc(yo_ready, 1)

            def y_stored(s, par):
                return s * 8 - 8 * par

            gelu(0, 0, first=True)
            gelu(1, 1, first=True)
            answer(0, 0, first=True)
            gelu(2, 0)
            answer(1, 1, first=True)
            with act.Fori(1, NSLOT // 2 - 1) as q:
                gelu(q * 2 + 1, 1)
                answer(q * 2, 0)
                gelu(q * 2 + 2, 0)
                answer(q * 2 + 1, 1)
            gelu(NSLOT - 1, 1)
            answer(NSLOT - 2, 0)
            answer(NSLOT - 1, 1)

        @block.tensor
        def _(pe):
            pe.wait_ge(pool_c, 4)
            pe.wait_ge(emb_w_in, 16 * 4)
            with pe.Fori(0, ROUNDS) as i:
                pe.wait_ge(xp_in, 16 * i + 16)
                pe.wait_ge(xsq_ready, i + 1)
                for q in range(4):
                    if q >= 2:
                        pe.wait_ge(img_sb, i * 4 + q - 1)
                    if q == 3:
                        pe.wait_ge(rowr_ready, i + 1)
                    c0 = IMG_T[q][1]
                    for k in range(KP):
                        nc.tensor.matmul(bank[q % 2][0:NIMG, 0:D], xp_s[:, k, c0:c0 + NIMG], tokw_s[:, k, :],
                                         start=(k == 0), stop=(k == KP - 1))
                    for k in range(KP):
                        last = nc.tensor.matmul(bank[q % 2][0:NIMG, D:D + 1], xsq[:, k, c0:c0 + NIMG], ones[:],
                                                start=(k == 0), stop=(k == KP - 1))
                    last.then_inc(img_mm, 1)
                for g in range(2):
                    for j in range(4):
                        last = nc.tensor.transpose(bank[2 + g][0:BASIN, 128 * j:128 * j + 128],
                                                   rowr[:, 4 * g + j, :], ident[:])
                    last.then_inc(rowt_mm, 1)
                for j in range(PAIR * 4):
                    pe.wait_ge(rowt_ready, i * 2 + j // 4 + 1)
                    last = nc.tensor.matmul(bank[4 + j // 2][:, (j % 2) * D:(j % 2) * D + D], rowt[:, j, :],
                                            projt_s[:], start=True, stop=True)
                    if j % 2:
                        last.then_inc(emb_mm, 1)

                def transposes(n):
                    for g in range(NG):
                        b, t0, t1, c0, _ = TRG[g // 2]
                        f0, fn = (0, DA) if g % 2 == 0 else (DA, DB)
                        for t in range(t0, t1):
                            if g % 2 == 0:
                                pe.wait_ge(nrm_ready, (i * LN + n) * NALL + b * NTILE + t + 1)
                            off, p = TILES[t]
                            last = nc.tensor.transpose(bank[g][0:fn, off - c0:off - c0 + p],
                                                       (nrm, nrm2)[n][0:p, b * NTILE + t, f0:f0 + fn], ident[0:p, 0:p])
                        last.then_inc(tr_mm, 1)

                transposes(0)
                pe.wait_ge(att_w_in, 16 * 3)
                for n in range(NKVR):
                    (m, l), half = KVR[n // 2], n % 2
                    pe.wait_ge(xm_ready, i * 9 + 3 * m + 3)
                    if n >= 8:
                        pe.wait_ge(kvr_ready, i * NKVR + n - 7)
                    cols = slice(half * MOVE, half * MOVE + MOVE)
                    outs = [(l, 0, DA, 0)] if l < 2 else [(b, DA, D, DB * b) for b in range(PAIR)]
                    for b, o0, o1, at in outs:
                        dst = bank[n % 8][at:at + o1 - o0, 0:MOVE]
                        nc.tensor.matmul(dst, attwa_s[:, m, o0:o1], xm[:, m, b, cols], start=True, stop=False)
                        last = nc.tensor.matmul(dst, attwb_s[DB * b:DB * b + DB, m, o0:o1],
                                                xm[DB * b:DB * b + DB, m, 2, cols], start=False, stop=True)
                    last.then_inc(kvr_mm, 1)
                for n, (b, t, off, p) in enumerate(ALL_T):
                    pe.wait_ge(ys_ready, i * 3 + 3)
                    if n >= 8:
                        pe.wait_ge(o_added, i * NALL + n - 7)
                    dst = bank[n % 8][0:p, 0:D]
                    nc.tensor.matmul(dst, ys[:, b, off:off + p], attwa_s[:, 3, :], start=True, stop=False)
                    nc.tensor.matmul(dst, ys[DB * b:DB * b + DB, 2, off:off + p], attwb_s[DB * b:DB * b + DB, 3, :],
                                     start=False, stop=True).then_inc(o_mm, 1)
                transposes(1)
                pe.wait_ge(tr_done, (i + 1) * LN * NG)
                pe.wait_ge(ffn_w_in, 16 * 6)
                for n, (b, t, off, p) in enumerate(ALL_T):
                    dst = bank[7][0:p, E * n:E * n + E]
                    nc.tensor.matmul(dst, na[:, b, off:off + p], wga_s[:], start=True, stop=False)
                    last = nc.tensor.matmul(dst, nb[:, b, off:off + p], wgb_s[:], start=False, stop=True)
                last.then_inc(gate_mm, 1)
                pe.wait_ge(mask_ready, i + 1)
                flat = rmask[:].rearrange("p e n -> p (e n)")
                nc.tensor.matmul(bank[7][:, 0:E * NALL], before[:], flat, start=True, stop=True)
                nc.tensor.matmul(bank[7][:, E * NALL:2 * E * NALL], all1[:], flat, start=True, stop=True)\
                    .then_inc(rank_mm, 1)
                pe.wait_ge(gate_ready, i + 1)
                for g in range(len(TRG)):
                    b, t0, t1, c0, _ = TRG[g]
                    for t in range(t0, t1):
                        off, p = TILES[t]
                        last = nc.tensor.transpose(bank[g][0:E, off - c0:off - c0 + p],
                                                   gate[0:p, b * NTILE + t, :], ident[0:p, 0:p])
                    last.then_inc(gt_mm, 1)
                pe.wait_ge(gt_ready, (i + 1) * len(TRG))
                for n, (b, t, off, p) in enumerate(ALL_T):
                    if n >= 3:
                        pe.wait_ge(bias_added, i * NALL + n - 2)
                    nc.tensor.matmul(bank[4 + n % 3][0:p, 0:D], gatet[:, b, off:off + p], b2_s[:],
                                     start=True, stop=True).then_inc(bias_mm, 1)

            def transpose_x(s, par, first=False):
                pe.wait_ge(x_in[par], s * 8 + 16 - 8 * par)
                if not first:
                    pe.wait_ge(xt_ready, s - 1)
                nc.tensor.transpose(bank[par][:, 0:128], xin[par][:, 0:DA], ident[:])
                nc.tensor.transpose(bank[par][0:DB, 128:256], xin[par][:, DA:D], ident[:]).then_inc(xt_mm, 1)

            def up(s, par, e, first=False):
                pe.wait_ge(xt_ready, s + 1)
                if not first:
                    pe.wait_ge(hid_ready, s - 1)
                dst = bank[2 + par][:, 0:H]
                nc.tensor.matmul(dst, xta[par], w1a_s[:, bass.ds(e, 1), :].rearrange("p o n -> p (o n)"),
                                 start=True, stop=False)
                nc.tensor.matmul(dst, xtb[par][0:DB + 1, :], w1b_s[:, bass.ds(e, 1), :].rearrange("p o n -> p (o n)"),
                                 start=False, stop=True).then_inc(up_mm, 1)

            def transpose_h(s, par, first=False):
                pe.wait_ge(hid_ready, s + 1)
                if not first:
                    pe.wait_ge(ht_ready, s - 1)
                for j in range(KH):
                    last = nc.tensor.transpose(bank[4 + par][:, 128 * j:128 * j + 128],
                                               hid[par][:, 128 * j:128 * j + 128], ident[:])
                last.then_inc(ht_mm, 1)

            def down(s, par, e, first=False):
                pe.wait_ge(ht_ready, s + 1)
                if not first:
                    pe.wait_ge(yo_ready, s - 1)
                for j in range(KH):
                    last = nc.tensor.matmul(bank[6 + par][:, 0:D], hidt[par][:, 128 * j:128 * j + 128],
                                            w2_s[:, bass.ds(e, 1), j, :].rearrange("p o n -> p (o n)"),
                                            start=(j == 0), stop=(j == KH - 1))
                last.then_inc(down_mm, 1)

            def expert(s):
                return pe.value_load(emap[0:1, bass.ds(s, 1)], min_val=0, max_val=E - 1)

            def step(s, par, first=False, first_down=False, next_up=True, next_x=True):
                e_down = expert(s - 1)
                e_up = expert(s + 1) if next_up else None
                down(s - 1, 1 - par, e_down, first=first_down)
                transpose_h(s, par, first=first)
                if next_up:
                    up(s + 1, 1 - par, e_up)
                if next_x:
                    transpose_x(s + 2, par)

            pe.wait_ge(emap_ready, ROUNDS)
            transpose_x(0, 0, first=True)
            up(0, 0, expert(0), first=True)
            transpose_x(1, 1, first=True)
            transpose_h(0, 0, first=True)
            up(1, 1, expert(1), first=True)
            transpose_x(2, 0)
            step(1, 1, first=True, first_down=True)
            step(2, 0, first_down=True)
            with pe.Fori(0, (NSLOT - 6) // UNROLL) as q:
                for u in range(UNROLL):
                    step(q * UNROLL + 3 + u, (3 + u) % 2)
            step(NSLOT - 3, 1)
            step(NSLOT - 2, 0, next_x=False)
            step(NSLOT - 1, 1, next_up=False, next_x=False)
            down(NSLOT - 1, 1, expert(NSLOT - 1))

        @block.vector
        def _(dve):
            V = nc.vector
            V.memset(x3[:, :, 0:1], 0.0)
            V.memset(slot0[:], 0.0)
            V.memset(osc[:, 0:1], -1e38).then_inc(o_mm, 1)
            V.memset(psc[:, 0:1], 0.0)
            V.memset(qsc[:, 0:1], 0.0)
            V.memset(sc[:], 0.0)
            V.memset(mv[:], 1.0)
            V.memset(eps_s[:, 0:1], LN_EPS)
            V.memset(eps_s[:, 1:2], RMS_EPS).then_inc(vec_c, 1)
            dve.wait_ge(ids_in, 16)
            V.tensor_scalar(idf[:, 0, :], ids_s[:], 0.0, float(VOCAB), op0=ALU.is_lt, op1=ALU.mult).then_inc(vec, 1)
            dve.wait_ge(vec, 1)
            V.tensor_tensor(idf[:, 1, :], ids_s[:], idf[:, 0, :], op=ALU.add).then_inc(vec, 1)
            dve.wait_ge(vec, 2)
            V.tensor_scalar(idc[:], idf[:, 1, :], 0.0, float(VOCAB - 1), op0=ALU.max, op1=ALU.min).then_inc(idc_ready, 1)
            dve.wait_ge(emb_w_in, 16 * 4)
            V.tensor_tensor_reduce(out=scr, in0=tokb_s[:], in1=tokb_s[:], scale=1.0, scalar=0.0,
                                   op0=ALU.mult, op1=ALU.add, accum_out=bsq[:, 0:1]).then_inc(vec, 1)
            dve.wait_ge(vec, 3)
            V.tensor_scalar_add(bsq[:, 1:2], bsq[:, 0:1], 1.0).then_inc(vec_c, 1)
            dve.wait_ge(att_w_in, 16 * 3)
            V.tensor_scalar(unmix[:], chan_s[:], -1.0, 1.0, op0=ALU.mult, op1=ALU.add).then_inc(vec_c, 1)
            dve.wait_ge(vec_c, 3)
            dve.wait_ge(pool_c, 11)
            PRE = 3
            with dve.Fori(0, ROUNDS) as i:
                steps = [0]

                def link(ins, alone=False):
                    steps[0] += 1
                    ins.then_inc(vec, 1)
                    dve.wait_ge(vec, i * VEC + PRE + steps[0])
                    if alone:
                        V.memset(carry[:], 0.0)

                b_img = tokb_s[0:NIMG, :]
                for q in range(4):
                    dve.wait_ge(img_mm, i * 4 + q + 1)
                    V.tensor_copy(mx[:, q, :], bank[q % 2][0:NIMG, 0:D + 1]).then_inc(img_sb, 1)
                    dve.wait_ge(img_sb, i * 4 + q + 1)
                    link(V.tensor_tensor_reduce(out=scr[0:NIMG, :], in0=mx[:, q, 0:D], in1=b_img, scale=1.0,
                                                scalar=0.0, op0=ALU.mult, op1=ALU.add, accum_out=st[:, 4, q:q + 1]))
                    V.tensor_reduce(st[:, 5, q:q + 1], mx[:, q, 0:D], axis=AX.X, op=ALU.max,
                                    apply_absolute_value=True)
                    if q == 1:
                        dve.wait_ge(rows_in, 16 * PAIR * 4 * (i + 1))
                        V.tensor_copy(rowr[:], rows[:, bass.ds(i * PAIR * 4, PAIR * 4), :]).then_inc(rowr_ready, 1)

                def row(n):
                    return st[:, n, :]

                V.tensor_copy(row(0), mx[:, :, D]).then_inc(a_vec, 1)
                dve.wait_ge(a_act, i * 4 + 1)
                link(V.tensor_scalar_max(st[:, 2:4, :], st[:, 2:4, :], EPS))
                link(V.tensor_scalar_min(row(6), row(2), ZMAX))
                link(V.tensor_scalar(row(7), row(6), -1.0, 1.0, op0=ALU.mult, op1=ALU.add))
                link(V.reciprocal(row(8), row(7)))
                link(V.scalar_tensor_tensor(row(6), row(6), 2.0, row(8), op0=ALU.mult, op1=ALU.mult))
                V.tensor_scalar_add(row(7), row(6), 1.0).then_inc(a_vec, 1)
                dve.wait_ge(a_vec, i * 4 + 2)
                link(V.tensor_scalar_add(row(11), row(7), -1.0))
                link(V.tensor_single_scalar(row(12), row(11), 0.0, op=ALU.is_equal))
                link(V.tensor_tensor(row(11), row(11), row(12), op=ALU.add))
                link(V.reciprocal(row(13), row(11)))
                dve.wait_ge(a_act, i * 4 + 2)
                link(V.tensor_tensor(row(8), row(8), row(12), op=ALU.add))
                link(V.tensor_tensor(row(8), row(8), row(6), op=ALU.mult))
                link(V.tensor_tensor(row(8), row(8), row(13), op=ALU.mult))
                link(V.reciprocal(row(14), row(2)))
                link(V.tensor_tensor(row(14), row(14), row(3), op=ALU.mult))
                V.tensor_tensor(row(9), row(14), row(8), op=ALU.mult).then_inc(a_vec, 1)
                link(V.reciprocal(row(15), row(3)))
                link(V.tensor_single_scalar(row(16), row(5), 0.0, op=ALU.is_gt))
                link(V.tensor_tensor(row(15), row(15), row(16), op=ALU.mult))
                for g in range(4):
                    dve.wait_ge(emb_mm, i * 4 + g + 1)
                    V.tensor_copy(emb[:, 2 * g:2 * g + 2, :], bank[4 + g][:, 0:2 * D].rearrange(
                        "p (j d) -> p j d", j=2)).then_inc(emb_sb, 1)
                dve.wait_ge(a_act, i * 4 + 3)
                link(V.tensor_tensor(row(15), row(15), row(10), op=ALU.mult))
                link(V.tensor_tensor(row(16), row(15), row(3), op=ALU.mult))
                link(V.tensor_scalar_max(row(16), row(16), EPS))
                link(V.reciprocal(row(17), row(16)))
                link(V.tensor_scalar(row(17), row(17), MAXNORM, 1.0, op0=ALU.mult, op1=ALU.min))
                link(V.tensor_tensor(row(15), row(15), row(17), op=ALU.mult))
                link(V.tensor_tensor(row(16), row(15), row(15), op=ALU.mult))
                link(V.tensor_tensor(row(16), row(16), row(1), op=ALU.mult))
                link(V.tensor_tensor(row(17), row(15), row(4), op=ALU.mult))
                link(V.tensor_scalar(row(18), row(17), 2.0, bsq[0:NIMG, 1:2], op0=ALU.mult, op1=ALU.add))
                link(V.tensor_scalar(row(17), row(17), 2.0, 1.0, op0=ALU.mult, op1=ALU.add))
                link(V.scalar_tensor_tensor(row(17), row(16), bsq[0:NIMG, 0:1], row(17), op0=ALU.mult, op1=ALU.add))
                link(V.tensor_scalar_max(row(17), row(17), EPS))
                link(V.reciprocal(row(19), row(17)))
                link(V.tensor_scalar(row(16), row(16), -1.0, 1.0, op0=ALU.mult, op1=ALU.add))
                link(V.tensor_tensor(row(16), row(16), row(19), op=ALU.mult))
                link(V.tensor_tensor(row(18), row(18), row(15), op=ALU.mult))
                link(V.tensor_tensor(row(18), row(18), row(19), op=ALU.mult))
                for q in range(4):
                    g = IMG_T[q][0]
                    link(V.tensor_scalar(hr(i, g, NIMG), b_img, st[:, 16, q:q + 1], None, op0=ALU.mult))
                    last = V.scalar_tensor_tensor(hr(i, g, NIMG), mx[:, q, 0:D], st[:, 18, q:q + 1],
                                                  hr(i, g, NIMG), op0=ALU.mult, op1=ALU.add)
                last.then_inc(a_vec, 1)
                dve.wait_ge(a_act, i * 4 + 4)
                link(V.tensor_scalar_max(row(21), row(21), EPS))
                link(V.reciprocal(row(22), row(21)))
                link(V.tensor_scalar(row(22), row(22), MAXNORM, 1.0, op0=ALU.mult, op1=ALU.min))
                for q in range(4):
                    g = IMG_T[q][0]
                    V.tensor_scalar(hr(i, g, NIMG), hr(i, g, NIMG), st[:, 22, q:q + 1], None, op0=ALU.mult)
                dve.wait_ge(rms_ready, i + 1)
                link(V.reciprocal(rin[:], rin[:]))
                for j, g in enumerate(TXT_T):
                    last = V.scalar_tensor_tensor(hr(i, g, 128), emb[:, j, :], rin[:, j:j + 1], normw_s[:],
                                                  op0=ALU.mult, op1=ALU.mult)
                link(last, alone=True)

                def layer_norm(n):
                    for g, (b, t, off, p) in enumerate(ALL_T):
                        last = V.bn_stats(bn[0:p, g, :], hr(i, g, p))
                    link(last, alone=True)
                    for g, (b, t, off, p) in enumerate(ALL_T):
                        last = V.bn_aggr(mv[0:p, g, :], bn[0:p, g, :])
                    last.then_inc(var_ready, 1)
                    dve.wait_ge(std_ready, i * LN + n + 1)
                    link(V.reciprocal(rstd[:], rstd[:]))
                    for g, (b, t, off, p) in enumerate(ALL_T):
                        V.tensor_scalar((nrm, nrm2)[n][0:p, g, :], hr(i, g, p), mv[0:p, g, 0:1], rstd[0:p, g:g + 1],
                                        op0=ALU.subtract, op1=ALU.mult).then_inc(nrm_ready, 1)

                layer_norm(0)
                dve.wait_ge(scattered, 16)
                dve.wait_ge(zeros_in, 16 * 3)
                dve.wait_ge(tr_done, (i * LN + 1) * NG)
                for m in range(3):
                    for l in range(3):
                        n = m * 3 + l
                        dve.wait_ge(z_ready, i * 9 + n + 1)
                        V.scalar_tensor_tensor(xm[:, m, l, :], x3[:, l, 1:T + 1], chan_s[:, 2 + m, l // 2:l // 2 + 1],
                                               zb[:, n % 2, :], op0=ALU.mult, op1=ALU.add).then_inc(xm_ready, 1)
                def got(m, l):
                    dve.wait_ge(kvr_ready, i * NKVR + 2 * KVR.index((m, l)) + 2)

                def differences(l):
                    k, w, u = kvr[:, 0, l, :], chan_s[:, 0, l // 2:l // 2 + 1], chan_s[:, 1, l // 2:l // 2 + 1]
                    got(0, l)
                    if l:
                        dve.wait_ge(dif_ready, i * 3 + l)
                    link(V.tensor_tensor_scan(osc[:, 1:T + 1], w.to_broadcast([128, T]), k, -1e38,
                                              op0=ALU.add, op1=ALU.max))
                    V.scalar_tensor_tensor(dif[:, 2 * (l % 2), :], osc[:, 0:T], w, k, op0=ALU.add, op1=ALU.subtract)
                    V.scalar_tensor_tensor(dif[:, 2 * (l % 2) + 1, :], k, u, osc[:, 0:T], op0=ALU.add, op1=ALU.subtract)\
                        .then_inc(dif_ready, 1)

                def sums(l):
                    g, (wkv, old, decay, now) = i * 3 + l, exl[l % 2]
                    got(1, l)
                    if l:
                        dve.wait_ge(ys_ready, g)
                    dve.wait_ge(ex_ready, g * 4 + 1)
                    link(V.tensor_tensor(bv[:], wkv, kvr[:, 1, l, :], op=ALU.mult))
                    dve.wait_ge(ex_ready, g * 4 + 2)
                    V.tensor_tensor_scan(psc[:, 1:T + 1], decay, bv[:], 0.0, op0=ALU.mult, op1=ALU.add)
                    link(V.tensor_tensor_scan(qsc[:, 1:T + 1], decay, wkv, 0.0, op0=ALU.mult, op1=ALU.add))
                    dve.wait_ge(ex_ready, g * 4 + 3)
                    V.tensor_tensor(num[:], old, psc[:, 0:T], op=ALU.mult)
                    link(V.tensor_tensor(den[:], old, qsc[:, 0:T], op=ALU.mult))
                    dve.wait_ge(ex_ready, g * 4 + 4)
                    link(V.tensor_tensor(den[:], den[:], now, op=ALU.add))
                    got(2, l)
                    link(V.scalar_tensor_tensor(den[:], kvr[:, 2, l, :], 1.0, den[:], op0=ALU.add, op1=ALU.mult))
                    dve.wait_ge(t2_ready, g + 1)
                    link(V.tensor_tensor(num[:], num[:], nu2[l % 2], op=ALU.add))
                    link(V.reciprocal(den[:], den[:]))
                    V.tensor_tensor(ys[:, l, :], num[:], den[:], op=ALU.mult).then_inc(ys_ready, 1)

                differences(0)
                differences(1)
                sums(0)
                differences(2)
                sums(1)
                sums(2)
                for n, (b, t, off, p) in enumerate(ALL_T):
                    dve.wait_ge(o_mm, i * NALL + n + 2)
                    V.tensor_tensor(hr(i, n, p), bank[n % 8][0:p, 0:D], hr(i, n, p), op=ALU.add).then_inc(o_added, 1)
                dve.wait_ge(o_added, (i + 1) * NALL)
                dve.wait_ge(scattered, i * 16 * NYG + 16)
                V.memset(carry[:], 0.0)
                layer_norm(1)
                dve.wait_ge(gate_mm, i + 1)
                for b in range(PAIR):
                    for p, t0, t1 in ((NIMG, 0, 2), (128, 2, NTILE)):
                        n0, n1 = b * NTILE + t0, b * NTILE + t1
                        last = V.tensor_copy(sc[0:p, n0:n1, :], bank[7][0:p, E * n0:E * n1].rearrange(
                            "p (n e) -> p n e", e=E))
                link(last, alone=True)
                for n in range(NALL):
                    last = V.max(m8[:, n, :], sc[:, n, :])
                link(last, alone=True)
                for n in range(NALL):
                    last = V.max_index(i8[:, n, :], m8[:, n, :], sc[:, n, :])
                V.tensor_tensor(pr[:, 0, :], m8[:, :, 1], m8[:, :, 0], op=ALU.subtract).then_inc(gap_ready, 1)
                link(last)
                link(V.tensor_copy(ixf[:], i8[:, :, 0:2]))
                both = [128, E, NALL]
                for s in range(K):
                    link(V.tensor_tensor(oh[:, s], ixf[:, :, s].rearrange("p (o n) -> p o n", o=1).to_broadcast(both),
                                         eiota[:].rearrange("p (e o) -> p e o", o=1).to_broadcast(both), op=ALU.is_equal))
                dve.wait_ge(e2_ready, i + 1)
                link(V.tensor_scalar_add(pr[:, 2, :], pr[:, 1, :], 1.0))
                link(V.reciprocal(pr[:, 2, :], pr[:, 2, :]))
                link(V.tensor_tensor(pr[:, 3, :], pr[:, 1, :], pr[:, 2, :], op=ALU.mult))
                for s in range(K):
                    link(V.tensor_tensor(ohw[:, s], oh[:, s],
                                         pr[:, 2 + s, :].rearrange("p (o n) -> p o n", o=1).to_broadcast(both), op=ALU.mult))
                V.tensor_tensor(gate[:].rearrange("p n e -> p e n"), ohw[:, 0], ohw[:, 1], op=ALU.add)\
                    .then_inc(gate_ready, 1)
                link(V.tensor_tensor(rmask[:], oh[:, 0], oh[:, 1], op=ALU.add))
                V.tensor_tensor(rmask[:], rmask[:], vmask[:].rearrange("p (o n) -> p o n", o=1).to_broadcast(both),
                                op=ALU.mult).then_inc(mask_ready, 1)
                V.tensor_copy(prob_all[:, bass.ds(i, 1)].rearrange("p o k n -> p (o k) n"), pr[:, 2:4, :])
                dve.wait_ge(rank_mm, i + 1)
                def flat(ap):
                    return ap.rearrange("p e n -> p (e n)")

                total, sums, slot, prod = (cnt[:, n] for n in range(4))
                link(V.tensor_copy(flat(total), bank[7][:, E * NALL:2 * E * NALL]))
                link(V.tensor_tensor_scan(flat(sums), ones[:].to_broadcast([128, E * NALL]), flat(total), 0.0,
                                          op0=ALU.mult, op1=ALU.add))
                link(V.tensor_tensor(sums, sums, total, op=ALU.subtract))
                link(V.tensor_reduce(per_e[:, 0, :], total, axis=AX.X, op=ALU.add))
                over_s = [128, E, EXP_TILES]
                link(V.tensor_tensor(over[:], per_e[:, 0, :].rearrange("p (e o) -> p e o", o=1).to_broadcast(over_s),
                                     thr[:].rearrange("p (o j) -> p o j", o=1).to_broadcast(over_s), op=ALU.is_gt))
                link(V.tensor_reduce(per_e[:, 1, :], over[:], axis=AX.X, op=ALU.add))
                link(V.tensor_tensor_scan(per_e[:, 2, :], ones[:].to_broadcast([128, E]), per_e[:, 1, :], 0.0,
                                          op0=ALU.mult, op1=ALU.add))
                link(V.tensor_tensor(per_e[:, 3, :], per_e[:, 2, :], per_e[:, 1, :], op=ALU.subtract))
                link(V.scalar_tensor_tensor(per_e[:, 4, :], per_e[:, 3, :], 128.0, sums[:, :, 0],
                                            op0=ALU.mult, op1=ALU.subtract))
                link(V.tensor_scalar(per_e[:, 4, :], per_e[:, 4, :], slot0[:], None, op0=ALU.add))
                link(V.tensor_tensor(flat(slot), flat(sums), bank[7][:, 0:E * NALL], op=ALU.add))
                link(V.tensor_tensor(slot, slot, per_e[:, 4, :].rearrange("p (e o) -> p e o", o=1).to_broadcast(both),
                                     op=ALU.add))
                for k in range(K):
                    link(V.tensor_tensor(prod, slot, oh[:, k], op=ALU.mult))
                    link(V.tensor_reduce(posf[:, k, :], prod.rearrange("p e n -> p n e"), axis=AX.X, op=ALU.add))
                V.tensor_copy(pos[:], posf[:].rearrange("p k n -> p (k n)")).then_inc(pos_ready, 1)
                V.tensor_copy(pos_all[:, bass.ds(i, 1)].rearrange("p o c -> p (o c)"), posf[:].rearrange("p k n -> p (k n)"))
                le_s = [1, SLOT_TILES, E]
                link(V.tensor_tensor(le, per_e[0:1, 2, :].rearrange("p (o e) -> p o e", o=1).to_broadcast(le_s),
                                     siota[:].rearrange("p (s o) -> p s o", o=1).to_broadcast(le_s), op=ALU.is_le))
                link(V.tensor_reduce(emf[:], le, axis=AX.X, op=ALU.add))
                V.tensor_scalar_min(emap[:, bass.ds(i * SLOT_TILES, SLOT_TILES)], emf[:], float(E - 1))\
                    .then_inc(emap_ready, 1)
                link(V.tensor_scalar_add(slot0[:], slot0[:], float(SLOT_TILES * 128)))
                for n, (b, t, off, p) in enumerate(ALL_T):
                    dve.wait_ge(bias_mm, i * NALL + n + 1)
                    V.tensor_tensor(hr(i, n, p), bank[4 + n % 3][0:p, 0:D], hr(i, n, p), op=ALU.add)\
                        .then_inc(bias_added, 1)
                dve.wait_ge(bias_added, (i + 1) * NALL)
                assert steps[0] == VEC, steps[0]

            V.memset(xtb[0][DB:DB + 1, :], 1.0)
            V.memset(xtb[1][DB:DB + 1, :], 1.0)
            V.tensor_copy(posg[:], pos_all[:]).then_inc(posg_ready, 1)

            def x_out(s, par, first=False):
                dve.wait_ge(xt_mm, s + 1)
                if not first:
                    dve.wait_ge(up_mm, s - 1)
                V.tensor_copy(xta[par], bank[par][:, 0:128])
                V.tensor_copy(xtb[par][0:DB, :], bank[par][0:DB, 128:256]).then_inc(xt_ready, 1)

            def h_out(s, par, first=False):
                dve.wait_ge(ht_mm, s + 1)
                if not first:
                    dve.wait_ge(down_mm, s - 1)
                V.tensor_copy(hidt[par], bank[4 + par][:, 0:H]).then_inc(ht_ready, 1)

            x_out(0, 0, first=True)
            x_out(1, 1, first=True)
            h_out(0, 0, first=True)
            x_out(2, 0)
            h_out(1, 1, first=True)
            with dve.Fori(1, NSLOT // 2 - 1) as q:
                x_out(q * 2 + 1, 1)
                h_out(q * 2, 0)
                x_out(q * 2 + 2, 0)
                h_out(q * 2 + 1, 1)
            x_out(NSLOT - 1, 1)
            h_out(NSLOT - 2, 0)
            h_out(NSLOT - 1, 1)
            for i in range(ROUNDS):
                dve.wait_ge(gathered[i], 16 * NYG)
                for k in range(K):
                    if k:
                        dve.wait_ge(y_added, i * K * NALL + NALL)
                    for n, (b, t, off, p) in enumerate(ALL_T):
                        g = i * NALL + n
                        V.scalar_tensor_tensor(h[0:p, g, :], yg[i][0:p, k * NALL + n, :], prob_all[0:p, i, k, n:n + 1],
                                               h[0:p, g, :], op0=ALU.mult, op1=ALU.add).then_inc(y_added, 1)
                dve.wait_ge(y_added, (i + 1) * K * NALL)
                V.memset(carry[:], 0.0).then_inc(h_final, 1)


_INS = [("xp", (128, KP, B * NP_)), ("tokw", (128, KP, D)), ("tokb", (D,)), ("ids", (128, B * 4)),
        ("basin", (VOCAB, BASIN)), ("projt", (BASIN, D)), ("normw", (D,)), ("chan", (128, 5, 2)),
        ("attwa", (128, 4, D)), ("attwb", (128, 4, D)), ("w1a", (DA, E, H)), ("w1b", (DB + 1, E, H)),
        ("w2", (128, E, KH, D)), ("b2", (E, D)), ("wga", (DA, E)), ("wgb", (DB, E))]


def kernel(x, x_txt, L0_tok_W, L0_tok_b, L0_txt_basin_coords, L0_txt_proj_w, L0_txt_norm_w,
           L0_attn_time_decay, L0_attn_time_first, L0_attn_time_mix_k, L0_attn_time_mix_v, L0_attn_time_mix_r,
           L0_attn_Wk, L0_attn_Wv, L0_attn_Wr, L0_attn_Wo,
           L0_ffn_Wg, L0_ffn_W1, L0_ffn_b1, L0_ffn_W2, L0_ffn_b2):
    import numpy as np
    import concourse.bacc as bacc
    from concourse.bass_utils import run_bass_kernel_spmd

    side = HW // PATCH
    pix = np.asarray(x).reshape(B, CH, side, PATCH, side, PATCH).transpose(1, 3, 5, 0, 2, 4).reshape(KP, 128, B * NP_)
    chan = [np.asarray(a).reshape(D) for a in (L0_attn_time_decay, L0_attn_time_first, L0_attn_time_mix_k,
                                               L0_attn_time_mix_v, L0_attn_time_mix_r)]
    att = np.stack([np.asarray(a).T for a in (L0_attn_Wk, L0_attn_Wv, L0_attn_Wr, L0_attn_Wo)], axis=1)
    w1, w2, wg = np.asarray(L0_ffn_W1), np.asarray(L0_ffn_W2), np.asarray(L0_ffn_Wg)
    data = {
        "xp": pix.transpose(1, 0, 2),
        "tokw": np.asarray(L0_tok_W).T.reshape(KP, 128, D).transpose(1, 0, 2),
        "tokb": np.asarray(L0_tok_b),
        "ids": np.asarray(x_txt).reshape(B * 4, 128).T,
        "basin": np.asarray(L0_txt_basin_coords),
        "projt": np.asarray(L0_txt_proj_w).T,
        "normw": np.asarray(L0_txt_norm_w),
        "chan": np.stack([np.stack([a[:DA], np.concatenate([a[DA:], a[DA:]])], axis=1) for a in chan], axis=1),
        "attwa": att[:DA], "attwb": np.concatenate([att[DA:], att[DA:]]),
        "w1a": w1[:, :DA].transpose(1, 0, 2), "w1b": np.concatenate([w1[:, DA:], np.asarray(L0_ffn_b1)[:, None]], axis=1).transpose(1, 0, 2),
        "w2": w2.reshape(E, KH, 128, D).transpose(2, 0, 1, 3),
        "b2": np.asarray(L0_ffn_b2),
        "wga": wg[:DA], "wgb": wg[DA:],
    }
    nc = bacc.Bacc("TRN2", target_bir_lowering=False, num_devices=1)
    arrays, args = {}, []
    for name, shape in _INS:
        a = np.ascontiguousarray(data[name])
        assert a.shape == shape, (name, a.shape)
        arrays[name] = a
        args.append(nc.dram_tensor(name, a.shape, mybir.dt.from_np(a.dtype), kind="ExternalInput").ap())
    args.append(nc.dram_tensor("out", (B, T, D), mybir.dt.float32, kind="ExternalOutput").ap())
    for name in ("slot_x", "slot_y"):
        args.append(nc.dram_tensor(name, (SLOTS, D), mybir.dt.float32, kind="Internal").ap())
    build(nc, *args)
    r = run_bass_kernel_spmd(nc, [arrays], core_ids=[0])
    return r.results[0]["out"]
```

```python
import concourse.bass as bass
from concourse import mybir
from contextlib import ExitStack

B, CH, HW, PATCH = 4, 3, 224, 16
D, PD, BASIN, VOCAB = 192, CH * PATCH * PATCH, 64, 32000
NP_, NT = (HW // PATCH) ** 2, 512
T = NP_ + NT
E, H = 8, 384
DA, DB = 128, D - 128
PAIR = 2
ROUNDS = B // PAIR
KP, KH, MOVE = PD // 128, H // 128, T // 2
TILES = [(0, NP_ // 2), (NP_ // 2, NP_ // 2)] + [(NP_ + 128 * j, 128) for j in range(NT // 128)]
NTILE = len(TILES)
NIMG = NP_ // 2
K = 2
EXP_TILES = -(-PAIR * T // 128)
SLOT_TILES = (K * PAIR * T + E * 127) // 128
SLOTS = SLOT_TILES * ROUNDS * 128
EPS, LN_EPS, RMS_EPS, MAXNORM = 1e-15, 1e-5, 1e-8, 1.0 - 0.004
ZMAX = 1.0 - 1e-7
ROW = D + 2
NOWHERE = 65536.0


def build(nc, xp, tokw, tokb, ids, basin, projt, normw, chan, attwa, attwb,
          w1a, w1b, w2, b2, wga, wgb, out, slot_x, answers):
    fp32, i32, u32 = mybir.dt.float32, mybir.dt.int32, mybir.dt.uint32
    ALU, ACT, AX = mybir.AluOpType, mybir.ActivationFunctionType, mybir.AxisListType
    ctx = ExitStack()
    with ctx:
        def sb(name, shape, dt=fp32):
            return ctx.enter_context(nc.sbuf_tensor(name, shape, dt))

        def sem(name):
            return ctx.enter_context(nc.semaphore(name))

        ident = sb("ident", [128, 128])
        ones = sb("ones", [128, 1])
        eiota = sb("eiota", [128, E])
        tokw_s = sb("tokw_s", [128, KP, D])
        tokb_s = sb("tokb_s", [128, D])
        normw_s = sb("normw_s", [128, D])
        projt_s = sb("projt_s", [BASIN, D])
        chan_s = sb("chan_s", [128, 5, 2])
        unmix = sb("unmix", [128, 5, 2])
        attwa_s = sb("attwa_s", [128, 4, D])
        attwb_s = sb("attwb_s", [128, 4, D])
        w1ah, w1al = sb("w1ah", [DA, E, H]), sb("w1al", [DA, E, H])
        w1bh, w1bl = sb("w1bh", [DB + 1, E, H]), sb("w1bl", [DB + 1, E, H])
        xth, xtl, xbh, xbl = (sb(name, [128, 2, 128]) for name in ("xth", "xtl", "xbh", "xbl"))
        w2_s = sb("w2_s", [128, E, KH, D])
        b2_s = sb("b2_s", [E, D])
        wga_s = sb("wga_s", [DA, E])
        wgb_s = sb("wgb_s", [DB, E])
        eps_s = sb("eps_s", [128, 2])
        bsq = sb("bsq", [128, 2])

        ids_s = sb("ids_s", [128, B * 4], i32)
        idf = sb("idf", [128, 2, B * 4])
        idc = sb("idc", [128, B * 4], u32)
        rows = sb("rows", [128, B * 4, BASIN])
        st = sb("st", [NIMG, 24, 2 * B])
        ss = sb("ss", [128, B * 4])
        rin = sb("rin", [128, B * 4])
        h = sb("h", [128, B * NTILE, D])
        nrm2 = sb("nrm2", [128, PAIR * NTILE, ROW])
        mx = nrm2[:].rearrange("p n d -> p (n d)")[:, 0:2 * B * (D + 1)].rearrange("p (q d) -> p q d", d=D + 1)
        place = sb("place", [128, PAIR * NTILE])
        bn = sb("bn", [128, PAIR * NTILE, 6])
        mv = sb("mv", [128, PAIR * NTILE, 2])
        rstd = sb("rstd", [128, PAIR * NTILE])
        x3 = sb("x3", [128, 3, T + 1])
        xm = sb("xm", [128, 3, 3, T])
        kvr = sb("kvr", [128, 3, 3, T])
        kvrf, xmf = (x[:].rearrange("p m l t -> p (m l t)") for x in (kvr, xm))
        xss = xmf[:, KP * B * NP_:(KP + 1) * B * NP_]
        xp_s, xsq = (f[:, 0:KP * B * NP_].rearrange("p (k c) -> p k c", k=KP) for f in (kvrf, xmf))
        osc = x3[:, 1, :]
        psc = sb("psc", [128, T + 1])
        qsc = sb("qsc", [128, T + 1])
        exdif = sb("exdif", [128, 8, T])
        ex, dif = exdif[:, 0:4], exdif[:, 4:8]
        w1raw = [f[:, a:a + E * H].rearrange("p (e n) -> p e n", e=E)
                 for f, a in ((kvrf, 3 * T), (exdif[:].rearrange("p s t -> p (s t)"), 0))]
        exf = ex.rearrange("p s t -> p (s t)")
        rowt = exf[0:BASIN, 0:B * 4 * 128].rearrange("p (j n) -> p j n", n=128)
        nrm = exf[:, 0:PAIR * NTILE * D].rearrange("p (n d) -> p n d", d=D)
        zb = [psc[:, 1:T + 1], qsc[:, 1:T + 1]]
        exl = [[ex[:, s, :] for s in range(4)],
               [xm[:, 0, 0, :], xm[:, 0, 1, :], xm[:, 0, 2, :], xm[:, 1, 0, :]]]
        bv, num, den = ([[dif[:, 0, :], dif[:, 2, :]]] + [[dif[:, 1, :], dif[:, 3, :]]] + [[exl[0][0], exl[1][0]]])
        nu2 = ys = kvr[:, 0]
        na, nb, gatet = xm[:, 0, 0:PAIR, :], xm[0:DB, 1, 0:PAIR, :], xm[0:E, 2, 0:PAIR, :]
        sc = sb("sc", [128, PAIR * NTILE, E])
        i8 = sb("i8", [128, PAIR * NTILE, 8], u32)
        ixf = sb("ixf", [128, PAIR * NTILE, 2])
        pr = sb("pr", [128, 4, PAIR * NTILE])
        NALL, NSLOT = PAIR * NTILE, ROUNDS * SLOT_TILES
        NE, at = PAIR * NTILE * E, E * H - 4 * T
        spare = []
        for width in (K * NE, K * NE, NE, NE, 4 * NE, E * EXP_TILES, NALL * 8, 5 * E, K * NALL):
            spare.append(dif.rearrange("p s t -> p (s t)")[:, at:at + width])
            at += width
        m8 = spare[6].rearrange("p (n e) -> p n e", n=NALL)
        oh, ohw = (a.rearrange("p (k e n) -> p k e n", k=K, e=E) for a in spare[:2])
        gate = spare[2].rearrange("p (n e) -> p n e", e=E)
        vmask = sb("vmask", [128, PAIR * NTILE])
        before = sb("before", [128, 128])
        all1 = sb("all1", [128, 128])
        thr = sb("thr", [128, EXP_TILES])
        siota = sb("siota", [128, SLOT_TILES])
        rmask = spare[3].rearrange("p (e n) -> p e n", e=E)
        cnt = spare[4].rearrange("p (a e n) -> p a e n", a=4, e=E)
        per_e = spare[7].rearrange("p (a e) -> p a e", a=5)
        over = spare[5].rearrange("p (e j) -> p e j", e=E)
        le = cnt[:].rearrange("p a e n -> p (a e n)")[:, 0:SLOT_TILES * E].rearrange("p (s e) -> p s e", e=E)
        emf = normw_s[:, 0:NSLOT]
        slot0 = sb("slot0", [128, 1])
        posf = spare[8].rearrange("p (k n) -> p k n", k=K)
        emap = sb("emap", [1, ROUNDS * SLOT_TILES], i32)
        pos = sb("pos", [128, ROUNDS, K * PAIR * NTILE], u32)
        prob_all = normw_s[:, NSLOT:NSLOT + ROUNDS * K * NALL].rearrange("p (i k n) -> p i k n", i=ROUNDS, k=K)
        def pairs_of(store, *widths):
            out, at = [], 0
            for w in widths:
                out.append([store[:, at + n * w:at + (n + 1) * w] for n in range(2)])
                at += 2 * w
            return out

        hid, yo = pairs_of(tokw_s[:].rearrange("p k d -> p (k d)"), H, D)
        hidt1 = sb("hidt1", [128, H])
        rowsf = rows[:].rearrange("p j d -> p (j d)")
        xin, hidt = [rowsf[:, 0:ROW], rowsf[:, ROW:2 * ROW]], [rowsf[:, 2 * ROW:2 * ROW + H], hidt1[:]]
        dest = sb("dest", [128, 4], u32)
        carry = sb("carry", [1, 1])
        NYG = K * PAIR * NTILE
        yg = [f[:, 0:NYG * D].rearrange("p (n k d) -> p n k d", k=K, d=D) for f in (xmf, kvrf)]
        NCLEAR = 5
        NZ = NSLOT // NCLEAR
        assert NZ * NCLEAR == NSLOT
        scr, scra = (dif.rearrange("p s t -> p (s t)")[:, at:at + D]
                     for at in (NZ * ROW, NZ * ROW + D))
        filler = dif.rearrange("p s t -> p (s t)")[:, 0:NZ * ROW]

        bank = [ctx.enter_context(nc.psum_tensor(f"bank{n}", [128, 512], fp32)) for n in range(8)]

        ids_in, emb_w_in, att_w_in, ffn_w_in = sem("ids_in"), sem("emb_w_in"), sem("att_w_in"), sem("ffn_w_in")
        xp_in, rows_in, out_done = [sem("xp_in0"), sem("xp_in1")], sem("rows_in"), [sem("out_done0"), sem("out_done1")]
        pool_c, vec_c, idc_ready = sem("pool_c"), sem("vec_c"), sem("idc_ready")
        vec = sem("vec")
        xsq_ready, xss_ready, img_mm, img_sb, img_S = sem("xsq_ready"), sem("xss_ready"), sem("img_mm"), sem("img_sb"), sem("img_S")
        sum_ready, a_act, a_vec = sem("sum_ready"), sem("a_act"), sem("a_vec")
        rowt_mm, rowt_ready = sem("rowt_mm"), sem("rowt_ready")
        emb_mm, emb_sb, ss_ready, rms_ready = sem("emb_mm"), sem("emb_sb"), sem("ss_ready"), sem("rms_ready")
        var_ready, std_ready, nrm_ready = sem("var_ready"), sem("std_ready"), sem("nrm_ready")
        tr_mm, tr_done = sem("tr_mm"), sem("tr_done")
        z_ready, z_used, xm_ready, kvr_mm, kvr_ready = (sem("z_ready"), sem("z_used"), sem("xm_ready"),
                                                        sem("kvr_mm"), sem("kvr_ready"))
        dif_ready, relu_ready, ex_ready, psc_ready, num_parts, num_ready, ys_ready = (sem("dif_ready"), sem("relu_ready"),
                                                               sem("ex_ready"), sem("psc_ready"), sem("num_parts"), sem("num_ready"), sem("ys_ready"))
        o_mm, o_added = sem("o_mm"), sem("o_added")
        gate_mm, gap_ready, e2_ready, gate_ready = sem("gate_mm"), sem("gap_ready"), sem("e2_ready"), sem("gate_ready")
        gt_mm, gt_ready, bias_mm, bias_added = sem("gt_mm"), sem("gt_ready"), sem("bias_mm"), sem("bias_added")
        filler_set, filler_in, mask_ready, rank_mm = sem("filler_set"), sem("filler_in"), sem("mask_ready"), sem("rank_mm")
        pos_ready, scattered, emap_ready = sem("pos_ready"), sem("scattered"), sem("emap_ready")
        x_in = [sem("x_in0"), sem("x_in1")]
        y_out = [sem("y_out0"), sem("y_out1")]
        w1_in, split_ready, xh_ready = sem("w1_in"), sem("split_ready"), sem("xh_ready")
        xt_mm, xt_ready, up_mm, hid_ready = sem("xt_mm"), sem("xt_ready"), sem("up_mm"), sem("hid_ready")
        ht_mm, ht_ready, down_mm, yo_ready = sem("ht_mm"), sem("ht_ready"), sem("down_mm"), sem("yo_ready")
        y_added = sem("y_added")
        carried, h_final = sem("carried"), sem("h_final")
        answers_in = [[sem(f"answers_in{i}{b}") for b in range(PAIR)] for i in range(ROUNDS)]

        IMG_T = [(b * NTILE + t, b * NP_ + t * NIMG) for b in range(B) for t in range(2)]
        TXT_T = [b * NTILE + 2 + j for b in range(B) for j in range(4)]
        ALL_T = [(b, t, *TILES[t]) for b in range(PAIR) for t in range(NTILE)]
        TRG = [(b, t0, t1, TILES[t0][0], sum(TILES[t][1] for t in range(t0, t1)))
               for b in range(PAIR) for t0, t1 in ((0, 4), (4, 6))]
        LN = 2
        NG = 2 * len(TRG)
        LANES = [0, 2, 1]
        KVR = [(m, LANES[at]) for m, at in ((0, 0), (0, 1), (1, 0), (2, 0), (0, 2), (1, 1), (2, 1), (1, 2), (2, 2))]
        NKVR = len(KVR) * 2
        W0, W1, W2, W3, W4 = 24, (24, 20), 12, 8, 6
        UNROLL = 18
        LOAD_AT, STORE_AT = 36, 56
        ADD_AT = 46
        WITHIN, START, at = {}, 1, 1
        for where, n in (("sums", 10), ("project", 2), ("norm", 1), ("gate", 1), ("route", 1)):
            WITHIN[where] = range(at, at + n)
            at += n
        REST = at

        f32r = mybir.dt.float32r

        def r(ap):
            return ap.bitcast(f32r)

        block = ctx.enter_context(nc.Block())

        def hr(i, g, p):
            return h[0:p, i * NALL + g, :]

        def cleared(n):
            return slot_x[n * NZ * 128:(n + 1) * NZ * 128, :].rearrange("(p j) d -> p (j d)", p=128)

        def load_answers(eng, i, seqs):
            for par in range(2):
                eng.wait_ge(y_out[par], 16 * SLOT_TILES // 2 * (i + 1))
            for b in seqs:
                for t0, t1 in ((0, 2), (2, NTILE)):
                    (off, p), n = TILES[t0], t1 - t0
                    row = (i * PAIR + b) * T + off
                    src = answers[K * row:K * (row + n * p), :].rearrange("(t p k) d -> p t (k d)", p=p, k=K)
                    dst = yg[i][0:p, b * NTILE + t0:b * NTILE + t1].rearrange("p t k d -> p t (k d)")
                    eng.dma_start(dst, src).then_inc(answers_in[i][b], 16)

        def store_out(eng, i):
            eng.wait_ge(h_final, i + 1)
            for b in range(i * PAIR, (i + 1) * PAIR):
                for t0, t1 in ((0, 2), (2, NTILE)):
                    (off, p), n = TILES[t0], t1 - t0
                    dst = out[b:b + 1, off:off + n * p, :].rearrange("o (t p) d -> p (o t) d", p=p)
                    eng.dma_start(dst, h[0:p, b * NTILE + t0:b * NTILE + t1, :]).then_inc(out_done[i], 16)

        def gate_t(g):
            at = (0, 0, 0, TRG[1][4])[g]
            return bank[(0, 1, 2, 1)[g]][0:E, at:at + TRG[g][4]]

        TWOS = [(n, b, off, p) for n, (b, t, off, p) in enumerate(ALL_T) if n % 2 == 0]

        def h_two(i, n, p):
            return h[0:p, i * NALL + n:i * NALL + n + 2, :]

        def tr_place(g, cn):
            bk, at = ((0, 0), (1, 0), (2, 0), (2, 256))[g % 4]
            return bank[bk][:, at:at + cn]

        def two(j, p, ring):
            return bank[j % ring][0:p, 0:2 * D].rearrange("p (t d) -> p t d", t=2)

        @block.sync
        def _(sp):
            sp.dma_start(ids_s[:], ids).then_inc(ids_in, 16)
            for dst, src in ((tokw_s, tokw), (tokb_s, tokb.partition_broadcast(128)),
                             (normw_s, normw.partition_broadcast(128)), (projt_s, projt)):
                sp.dma_start(dst[:], src).then_inc(emb_w_in, 16)
            for dst, src in ((chan_s, chan), (attwa_s, attwa), (attwb_s, attwb)):
                sp.dma_start(dst[:], src).then_inc(att_w_in, 16)
            sp.wait_ge(rows_in, 16 * B * 4)
            for dst, src in ((w2_s, w2), (b2_s, b2), (wga_s, wga), (wgb_s, wgb)):
                sp.dma_start(dst[:], src).then_inc(ffn_w_in, 16)
            sp.wait_ge(filler_set, 1)
            for n in range(NCLEAR):
                sp.dma_start(cleared(n), filler).then_inc(filler_in, 16)

            sp.wait_ge(ys_ready, 3)
            sp.dma_start(w1raw[0], w1a).then_inc(w1_in, 16)
            sp.dma_start(w1raw[1][0:DB + 1], w1b).then_inc(w1_in, 16)

            def load(s, par, first=False):
                if not first:
                    sp.wait_ge(xt_ready, s - 1)
                sp.dma_start(xin[par], slot_x[bass.ds(s * 128, 128), :]).then_inc(x_in[par], 16)

            def loads(lo, hi):
                with sp.Fori(lo // 2, hi // 2) as q:
                    for par in range(2):
                        load(q * 2 + par, par)

            sp.wait_ge(scattered, 16 * NYG)
            load(0, 0, first=True)
            load(1, 1, first=True)
            load(2, 0)
            load(3, 1)
            loads(4, SLOT_TILES)
            sp.wait_ge(scattered, 16 * NYG * ROUNDS)
            loads(SLOT_TILES, LOAD_AT)
            load_answers(sp, 0, range(PAIR))
            loads(LOAD_AT, STORE_AT)
            store_out(sp, 0)
            loads(STORE_AT, NSLOT)
            for b in range(PAIR):
                load_answers(sp, ROUNDS - 1, [b])
            store_out(sp, ROUNDS - 1)
            for i in range(ROUNDS):
                sp.wait_ge(out_done[i], 16 * 2 * PAIR)

        @block.gpsimd
        def _(pool):
            nc.gpsimd.memset(ones[:], 1.0).then_inc(pool_c, 1)
            nc.gpsimd.memset(ident[:], 0.0).then_inc(pool_c, 1)
            nc.gpsimd.iota(eiota[:], [[1, E]], base=0, channel_multiplier=0,
                           allow_small_or_imprecise_dtypes=True).then_inc(pool_c, 1)
            pool.wait_ge(pool_c, 3)
            nc.gpsimd.affine_select(out=ident[:], in_=ident[:], compare_op=ALU.not_equal, fill=1.0, base=0,
                                    pattern=[[-1, 128]], channel_multiplier=1).then_inc(pool_c, 1)
            pool.wait_ge(idc_ready, 1)
            for j in range(B * 4):
                nc.gpsimd.indirect_dma_start(
                    out=rows[:, j, :], out_offset=None, in_=basin,
                    in_offset=bass.IndirectOffsetOnAxis(ap=idc[:, j:j + 1], axis=0)).then_inc(rows_in, 16)
            nc.gpsimd.memset(filler, NOWHERE).then_inc(filler_set, 1)
            nc.gpsimd.memset(all1[:], 1.0).then_inc(pool_c, 1)
            nc.gpsimd.memset(vmask[:], 1.0).then_inc(pool_c, 1)
            nc.gpsimd.iota(thr[:], [[128, EXP_TILES]], base=0, channel_multiplier=0,
                           allow_small_or_imprecise_dtypes=True).then_inc(pool_c, 1)
            nc.gpsimd.iota(siota[:], [[1, SLOT_TILES]], base=0, channel_multiplier=0,
                           allow_small_or_imprecise_dtypes=True).then_inc(pool_c, 1)
            pool.wait_ge(pool_c, 8)
            nc.gpsimd.affine_select(out=before[:], in_=all1[:], compare_op=ALU.is_gt, fill=0.0, base=0,
                                    pattern=[[1, 128]], channel_multiplier=-1).then_inc(pool_c, 1)
            for b in range(PAIR):
                for t0, n in ((0, 2), (2, NT // 128)):
                    nc.gpsimd.iota(place[:, b * NTILE + t0:b * NTILE + t0 + n], [[K * TILES[t0][1], n]],
                                   base=K * (b * T + TILES[t0][0]), channel_multiplier=K,
                                   allow_small_or_imprecise_dtypes=True).then_inc(pool_c, 1)
                cols = vmask[:, b * NTILE:b * NTILE + 2]
                nc.gpsimd.affine_select(out=cols, in_=cols, compare_op=ALU.is_gt, fill=0.0, base=NIMG,
                                        pattern=[[0, 2]], channel_multiplier=-1).then_inc(pool_c, 1)

            def scatter_rows(i, lo, hi):
                pool.wait_ge(pos_ready, i + 1)
                for n in range(lo, hi):
                    c, p = n % K * NALL + n // K, ALL_T[n // K][3]
                    nc.gpsimd.indirect_dma_start(
                        out=slot_x, out_offset=bass.IndirectOffsetOnAxis(ap=pos[0:p, i, c:c + 1], axis=0),
                        in_=nrm2[0:p, n // K, :], in_offset=None).then_inc(scattered, 16)

            def scatter_answers(s, par, col):
                pool.wait_ge(yo_ready, s + 1)
                if not isinstance(s, int):
                    pool.wait_ge(carried, s - first_in_loop + 1)
                    nc.gpsimd.tensor_tensor(carry[:], ones[0:1, :], ones[0:1, :], op=ALU.mult).then_inc(carried, 1)
                nc.gpsimd.indirect_dma_start(
                    out=answers, out_offset=bass.IndirectOffsetOnAxis(ap=dest[:, col:col + 1], axis=0),
                    in_=yo[par], in_offset=None, bounds_check=K * B * T - 1, oob_is_err=False).then_inc(y_out[par], 16)

            early = 4
            for i in range(ROUNDS):
                for at, l in enumerate(LANES):
                    g, (_, old, _, now) = i * 3 + at, exl[at % 2]
                    if i == ROUNDS - 1 and at == 2:
                        for s in range(early):
                            scatter_answers(s, s % 2, s % 4)
                    pool.wait_ge(kvr_ready, i * NKVR + 2 * KVR.index((1, l)) + 2)
                    pool.wait_ge(ex_ready, g * 4 + 4)
                    nc.gpsimd.tensor_tensor(nu2[:, l, :], now, kvr[:, 1, l, :], op=ALU.mult).then_inc(num_parts, 1)
                    pool.wait_ge(psc_ready, g + 1)
                    nc.gpsimd.tensor_tensor(num[at % 2], old, psc[:, 0:T], op=ALU.mult).then_inc(num_parts, 1)
                    pool.wait_ge(num_parts, 2 * g + 2)
                    nc.gpsimd.tensor_tensor(num[at % 2], num[at % 2], nu2[:, l, :], op=ALU.add).then_inc(num_ready, 1)
                if i == 0:
                    pool.wait_ge(filler_in, 16 * NCLEAR)
                    scatter_rows(i, 0, NYG)
            done = WITHIN["route"][0] - 1
            for s in range(early, done):
                scatter_answers(s, s % 2, s % 4)
            for n in range(0, NYG, 2):
                scatter_rows(1, n, n + 2)
                scatter_answers(done, done % 2, done % 4)
                done += 1
            assert done <= SLOT_TILES - 2
            turns, first_in_loop = (NSLOT - done) // 4, done
            nc.gpsimd.memset(carry[:], 0.0).then_inc(carried, 1)
            with pool.Fori(0, turns) as q:
                for u in range(4):
                    scatter_answers(q * 4 + done + u, (done + u) % 2, (done + u) % 4)
            for s in range(done + 4 * turns, NSLOT):
                scatter_answers(s, s % 2, s % 4)

        @block.scalar
        def _(act):
            def gelu(s, par, first=False):
                act.wait_ge(up_mm, s + 1)
                if not first:
                    act.wait_ge(ht_mm, s - 1)
                nc.scalar.activation(hid[par], bank[5][:, 0:H], ACT.Gelu).then_inc(hid_ready, 1)

            def answer(s, par, first=False):
                act.wait_ge(down_mm, s + 1)
                if not first:
                    act.wait_ge(y_out[par], s * 8 - 8 * par)
                nc.scalar.activation(yo[par], bank[7][:, par * D:par * D + D], ACT.Copy).then_inc(yo_ready, 1)

            def x_high(s, par, first=False):
                act.wait_ge(xt_mm, s + 1)
                if not first:
                    act.wait_ge(up_mm, s - 1)
                at = par * 256
                nc.scalar.activation(r(xth[:, par]), bank[4][:, at:at + 128], ACT.Copy)
                nc.scalar.activation(r(xbh[0:DB, par]), bank[4][0:DB, at + 128:at + 256], ACT.Copy).then_inc(xh_ready, 1)

            def slot_step(s, par, next_up=True, next_x=True):
                answer(s - 1, 1 - par, first=isinstance(s, int) and s <= 2)
                if next_x:
                    x_high(s + 2, par)
                if next_up:
                    gelu(s + 1, 1 - par)

            def slot_steps(where):
                for s in WITHIN[where]:
                    slot_step(s, s % 2)

            for n in range(ROUNDS):
                cols = slice(n * PAIR * NP_, (n + 1) * PAIR * NP_)
                act.dma_start(xp_s[:, :, cols], xp[:, :, cols]).then_inc(xp_in[n], 16)
            for n in range(ROUNDS):
                cols = slice(n * PAIR * NP_, (n + 1) * PAIR * NP_)
                act.wait_ge(xp_in[n], 16)
                nc.scalar.activation(xsq[:, :, cols], xp_s[:, :, cols], ACT.Square).then_inc(xsq_ready, 1)
            for q in range(2 * B):
                act.wait_ge(img_sb, q + 1)
                if q:
                    act.wait_ge(img_S, q)
                nc.scalar.activation(scra[0:NIMG, :], mx[0:NIMG, q, 0:D], ACT.Square,
                                     accum_out=st[:, 1, q:q + 1]).then_inc(img_S, 1)
                if q in (3, 4):
                    for g in (2 * q - 6, 2 * q - 5):
                        act.wait_ge(rowt_mm, g + 1)
                        nc.scalar.activation(rowt[:, 4 * g:4 * g + 4, :], bank[2 + g % 2][0:BASIN, :].rearrange(
                            "p (j n) -> p j n", j=4), ACT.Copy).then_inc(rowt_ready, 1)
            act.wait_ge(img_S, 2 * B)
            act.wait_ge(a_vec, 1)
            nc.scalar.activation(st[:, 2:4, :], st[:, 0:2, :], ACT.Sqrt).then_inc(a_act, 1)
            act.wait_ge(a_vec, 2)
            nc.scalar.activation(st[:, 8, :], st[:, 7, :], ACT.Ln).then_inc(a_act, 1)
            act.wait_ge(a_vec, 3)
            nc.scalar.activation(st[:, 10, :], st[:, 9, :], ACT.Tanh, scale=0.5).then_inc(a_act, 1)
            for j in range(B * 4):
                act.wait_ge(emb_sb, j // 2 + 1)
                if j:
                    act.wait_ge(ss_ready, j)
                nc.scalar.activation(scra, h[:, TXT_T[j], :], ACT.Square, accum_out=ss[:, j:j + 1]).then_inc(ss_ready, 1)
            act.wait_ge(ss_ready, B * 4)
            nc.scalar.activation(rin[:], ss[:], ACT.Sqrt, scale=1.0 / D, bias=eps_s[:, 1:2]).then_inc(rms_ready, 1)
            for q in range(2 * B):
                act.wait_ge(sum_ready, q + 1)
                act.wait_ge(img_S, 2 * B + q)
                nc.scalar.activation(scra[0:NIMG, :], h[0:NIMG, IMG_T[q][0], :], ACT.Square,
                                     accum_out=st[:, 20, q:q + 1]).then_inc(img_S, 1)
            act.wait_ge(img_S, 4 * B)
            nc.scalar.activation(st[:, 21, :], st[:, 20, :], ACT.Sqrt).then_inc(a_act, 1)

            for i in range(ROUNDS):
                within = i == ROUNDS - 1

                def deviations(n, b):
                    act.wait_ge(var_ready, (i * LN + n) * PAIR + b + 1)
                    these = slice(b * NTILE, (b + 1) * NTILE)
                    nc.scalar.activation(rstd[:, these], mv[:, these, 1], ACT.Sqrt, bias=eps_s[:, 0:1]).then_inc(std_ready, 1)

                def transposed(n, b, dst):
                    for g in range(4 * b, 4 * b + 4):
                        act.wait_ge(tr_mm, (i * LN + n) * NG + (g + 2 if g % 4 == 2 else g + 1))
                        _, _, _, c0, cn = TRG[g // 2]
                        nc.scalar.activation(dst(b, g % 2, c0, cn), tr_place(g, cn)[0:DA if g % 2 == 0 else DB],
                                             ACT.Copy).then_inc(tr_done, 1)

                for b in range(PAIR):
                    deviations(0, b)
                for b in range(PAIR):
                    transposed(0, b, lambda b, part, c0, cn:
                               x3[:, b, 1 + c0:1 + c0 + cn] if part == 0 else
                               x3[DB * b:DB * b + DB, 2, 1 + c0:1 + c0 + cn])
                act.wait_ge(tr_done, (i * LN + 1) * NG)
                act.wait_ge(vec_c, 3)
                for m in range(3):
                    for l in range(3):
                        n = m * 3 + l
                        if n >= 2:
                            act.wait_ge(xm_ready, i * 9 + n - 1)
                        nc.scalar.activation(zb[n % 2], x3[:, l, 0:T], ACT.Copy,
                                             scale=unmix[:, 2 + m, l // 2:l // 2 + 1]).then_inc(z_ready, 1)

                def evacuate(first, last):
                    for n in range(2 * first, 2 * last):
                        m, l = KVR[n // 2]
                        half = n % 2 * MOVE
                        act.wait_ge(kvr_mm, i * NKVR + n + 1)
                        nc.scalar.activation(kvr[:, m, l, half:half + MOVE], bank[n % 8][:, 0:MOVE],
                                             ACT.Exp if m == 2 else ACT.Copy,
                                             scale=-1.0 if m == 2 else 1.0).then_inc(kvr_ready, 1)

                def exponentials(at):
                    g = i * 3 + at
                    if at == 2:
                        act.wait_ge(ys_ready, g - 1)
                    if at == 1:
                        act.wait_ge(kvr_mm, i * NKVR + 16)
                    for n, (s, sign) in enumerate(((0, 1.0), (2, -1.0), (1, 1.0), (3, -1.0))):
                        dst = exl[at % 2][s]
                        act.wait_ge(dif_ready, g + 1)
                        nc.scalar.activation(dst, dif[:, 2 * (at % 2) + s % 2, :], ACT.Relu, scale=sign)\
                            .then_inc(relu_ready, 1)
                        act.wait_ge(relu_ready, g * 4 + n + 1)
                        nc.scalar.activation(dst, dst, ACT.Exp, scale=-1.0).then_inc(ex_ready, 1)

                evacuate(0, 2)
                exponentials(0)
                evacuate(2, 5)
                exponentials(1)
                evacuate(5, 9)
                exponentials(2)
                if within:
                    x_high(0, 0, first=True)
                    x_high(1, 1, first=True)
                    gelu(0, 0, first=True)
                    x_high(2, 0)
                    gelu(1, 1, first=True)
                    slot_steps("sums")
                for b in range(PAIR):
                    deviations(1, b)
                for b, where in enumerate(("project", "norm")):
                    if within:
                        slot_steps(where)
                    transposed(1, b, lambda b, part, c0, cn: (na if part == 0 else nb)[:, b, c0:c0 + cn])
                if within:
                    slot_steps("gate")
                act.wait_ge(gap_ready, i + 1)
                nc.scalar.activation(pr[:, 1, :], pr[:, 0, :], ACT.Exp).then_inc(e2_ready, 1)
                if within:
                    slot_steps("route")
                for g, (b, _, _, c0, cn) in enumerate(TRG):
                    act.wait_ge(gt_mm, (i + 1) * len(TRG))
                    nc.scalar.activation(gatet[:, b, c0:c0 + cn], gate_t(g), ACT.Copy).then_inc(gt_ready, 1)

            rest = (NSLOT - 2 - REST) // 2
            with act.Fori(0, rest) as q:
                for u in range(2):
                    slot_step(q * 2 + REST + u, (REST + u) % 2)
            for s in range(REST + 2 * rest, NSLOT):
                slot_step(s, s % 2, next_up=s < NSLOT - 1, next_x=s < NSLOT - 2)
            answer(NSLOT - 1, (NSLOT - 1) % 2)

        @block.tensor
        def _(pe):
            def transpose_x(s, par):
                pe.wait_ge(x_in[par], s * 8 + 16 - 8 * par)
                if not isinstance(s, int) or s:
                    pe.wait_ge(xt_ready, s)
                at = par * 256
                nc.tensor.transpose(bank[4][:, at:at + 128], xin[par][:, 0:DA], ident[:])
                nc.tensor.transpose(bank[4][0:DB, at + 128:at + 256], xin[par][:, DA:D], ident[:]).then_inc(xt_mm, 1)

            def up(s, par, e):
                pe.wait_ge(xt_ready, s + 1)
                xh, xl, one = xth[:, par], xtl[:, par], xbh[0:DB + 1, par]
                parts = ((xh, w1ah), (xl, w1ah), (xh, w1al), (one, w1bh), (xbl[0:DB, par], w1bh[0:DB]), (one, w1bl))
                for n, (x, w) in enumerate(parts):
                    last = nc.tensor.matmul(bank[5][:, 0:H], r(x), r(w[:, bass.ds(e, 1), :].rearrange("p o n -> p (o n)")),
                                            start=(n == 0), stop=(n == len(parts) - 1))
                last.then_inc(up_mm, 1)

            def transpose_h(s, par):
                pe.wait_ge(hid_ready, s + 1)
                for j in range(KH):
                    last = nc.tensor.transpose(bank[6][:, 128 * j:128 * j + 128],
                                               hid[par][:, 128 * j:128 * j + 128], ident[:])
                last.then_inc(ht_mm, 1)

            def down(s, par, e, first=False):
                pe.wait_ge(ht_ready, s + 1)
                if not first:
                    pe.wait_ge(yo_ready, s)
                for j in range(KH):
                    last = nc.tensor.matmul(bank[7][:, par * D:par * D + D], hidt[par][:, 128 * j:128 * j + 128],
                                            w2_s[:, bass.ds(e, 1), j, :].rearrange("p o n -> p (o n)"),
                                            start=(j == 0), stop=(j == KH - 1))
                last.then_inc(down_mm, 1)

            def expert(s):
                return pe.value_load(emap[0:1, bass.ds(s, 1)], min_val=0, max_val=E - 1)

            def slot_step(s, par, e, next_up=True, next_x=True, next_e=True):
                down(s - 1, 1 - par, e[0], first=isinstance(s, int) and s == 1)
                e_next = expert(s + 2) if next_e else None
                transpose_h(s, par)
                if next_x:
                    transpose_x(s + 2, par)
                if next_up:
                    up(s + 1, 1 - par, e[2])
                return e[1], e[2], e_next

            def slot_steps(where):
                e = [expert(s + d) for s in WITHIN[where][:1] for d in (-1, 0, 1)]
                for s in WITHIN[where]:
                    e = slot_step(s, s % 2, e, next_e=s != WITHIN[where][-1])

            def keep_busy(n):
                for _ in range(n):
                    nc.tensor.matmul(bank[4][:, 0:128], ident[:], ident[:], start=True, stop=True)

            pe.wait_ge(pool_c, 4)
            keep_busy(W0)
            pe.wait_ge(emb_w_in, 16 * 4)
            def rows_transposed(lo, hi):
                pe.wait_ge(rows_in, 16 * B * 4)
                for g in range(lo, hi):
                    if g >= 2:
                        pe.wait_ge(rowt_ready, g - 1)
                    for j in range(4):
                        last = nc.tensor.transpose(bank[2 + g % 2][0:BASIN, 128 * j:128 * j + 128],
                                                   rows[:, 4 * g + j, :], ident[:])
                    last.then_inc(rowt_mm, 1)

            def projected(lo, hi):
                for j in range(lo, hi):
                    pe.wait_ge(rowt_ready, j // 4 + 1)
                    if j >= 8 and j % 2 == 0:
                        pe.wait_ge(emb_sb, j // 2 - 3)
                    last = nc.tensor.matmul(bank[4 + j // 2 % 4][:, (j % 2) * D:(j % 2) * D + D], rowt[:, j, :],
                                            projt_s[:], start=True, stop=True)
                    if j % 2:
                        last.then_inc(emb_mm, 1)

            for q in range(2 * B):
                pe.wait_ge(xp_in[q // 4], 16)
                if q >= 2:
                    pe.wait_ge(img_sb, q - 1)
                c0 = IMG_T[q][1]
                for k in range(KP):
                    nc.tensor.matmul(bank[q % 2][0:NIMG, 0:D], xp_s[:, k, c0:c0 + NIMG], tokw_s[:, k, :],
                                     start=(k == 0), stop=(k == KP - 1))
                pe.wait_ge(xss_ready, q // 4 + 1)
                nc.tensor.matmul(bank[q % 2][0:NIMG, D:D + 1], xss[:, c0:c0 + NIMG], ones[:],
                                 start=True, stop=True).then_inc(img_mm, 1)
                if q in (3, 4):
                    rows_transposed(2 * (q - 3), 2 * (q - 2))
                if q in (5, 6):
                    projected(8 * (q - 5), 8 * (q - 4))

            for i in range(ROUNDS):
                within = i == ROUNDS - 1

                def transposes(n, b):
                    for g in range(4 * b, 4 * b + 4):
                        _, t0, t1, c0, cn = TRG[g // 2]
                        f0, fn = (0, DA) if g % 2 == 0 else (DA, DB)
                        if g >= 4 and g % 4 != 3:
                            pe.wait_ge(tr_done, (i * LN + n) * NG + (4 if g % 4 == 2 else g - 3))
                        for t in range(t0, t1):
                            if g % 2 == 0:
                                pe.wait_ge(nrm_ready, (i * LN + n) * NALL + b * NTILE + t + 1)
                            off, p = TILES[t]
                            last = nc.tensor.transpose(tr_place(g, cn)[0:fn, off - c0:off - c0 + p],
                                                       (nrm, nrm2)[n][0:p, b * NTILE + t, f0:f0 + fn], ident[0:p, 0:p])
                        last.then_inc(tr_mm, 1)

                if i == 0:
                    pe.wait_ge(emb_sb, 2 * B)
                    pe.wait_ge(a_act, 4)
                keep_busy(W1[i])
                transposes(0, 0)
                transposes(0, 1)
                keep_busy(W2)
                pe.wait_ge(att_w_in, 16 * 3)
                for n in range(NKVR):
                    (m, l), half = KVR[n // 2], n % 2
                    pe.wait_ge(xm_ready, i * 9 + 3 * m + 3)
                    if n >= 8:
                        pe.wait_ge(kvr_ready, i * NKVR + n - 7)
                    cols = slice(half * MOVE, half * MOVE + MOVE)
                    outs = [(l, 0, DA, 0)] if l < 2 else [(b, DA, D, DB * b) for b in range(PAIR)]
                    for b, o0, o1, at in outs:
                        dst = bank[n % 8][at:at + o1 - o0, 0:MOVE]
                        nc.tensor.matmul(dst, attwa_s[:, m, o0:o1], xm[:, m, b, cols], start=True, stop=False)
                        last = nc.tensor.matmul(dst, attwb_s[DB * b:DB * b + DB, m, o0:o1],
                                                xm[DB * b:DB * b + DB, m, 2, cols], start=False, stop=True)
                    last.then_inc(kvr_mm, 1)
                pe.wait_ge(kvr_ready, (i + 1) * NKVR)
                if within:
                    pe.wait_ge(emap_ready, ROUNDS - 1)
                    pe.wait_ge(split_ready, 1)
                    transpose_x(0, 0)
                    up(0, 0, expert(0))
                    transpose_x(1, 1)
                    transpose_h(0, 0)
                    transpose_x(2, 0)
                    up(1, 1, expert(1))
                    slot_steps("sums")
                else:
                    pe.wait_ge(psc_ready, (i + 1) * 3)
                    keep_busy(W3)
                for j, (n, b, off, p) in enumerate(TWOS):
                    pe.wait_ge(ys_ready, i * 3 + 2 + b)
                    if j >= 4:
                        pe.wait_ge(o_added, i * len(TWOS) + j - 3)
                    for t in range(2):
                        dst, tok = two(j, p, 4)[:, t, :], slice(off + t * p, off + t * p + p)
                        nc.tensor.matmul(dst, ys[:, b, tok], attwa_s[:, 3, :], start=True, stop=False)
                        last = nc.tensor.matmul(dst, ys[DB * b:DB * b + DB, 2, tok], attwb_s[DB * b:DB * b + DB, 3, :],
                                                start=False, stop=True)
                    last.then_inc(o_mm, 1)
                pe.wait_ge(ffn_w_in, 16 * 4)
                for b, where in enumerate(("project", "norm")):
                    if within:
                        slot_steps(where)
                    pe.wait_ge(o_added, (i + 1) * len(TWOS))
                    transposes(1, b)
                    pe.wait_ge(tr_done, (i * LN + 1) * NG + 4 * (b + 1))
                    for t, (off, p) in enumerate(TILES):
                        at = E * (b * NTILE + t)
                        dst = bank[3][0:p, at:at + E]
                        nc.tensor.matmul(dst, na[:, b, off:off + p], wga_s[:], start=True, stop=False)
                        last = nc.tensor.matmul(dst, nb[:, b, off:off + p], wgb_s[:], start=False, stop=True)
                last.then_inc(gate_mm, 1)
                if within:
                    slot_steps("gate")
                else:
                    keep_busy(W4)
                pe.wait_ge(mask_ready, i + 1)
                flat = rmask[:].rearrange("p e n -> p (e n)")
                nc.tensor.matmul(bank[3][:, 0:E * NALL], before[:], flat, start=True, stop=True)
                nc.tensor.matmul(bank[3][:, E * NALL:2 * E * NALL], all1[:], flat, start=True, stop=True)\
                    .then_inc(rank_mm, 1)
                pe.wait_ge(gate_ready, i + 1)
                for g, (b, t0, t1, c0, _) in enumerate(TRG):
                    for t in range(t0, t1):
                        off, p = TILES[t]
                        last = nc.tensor.transpose(gate_t(g)[:, off - c0:off - c0 + p],
                                                   gate[0:p, b * NTILE + t, :], ident[0:p, 0:p])
                    last.then_inc(gt_mm, 1)
                if within:
                    slot_steps("route")
                pe.wait_ge(gt_ready, (i + 1) * len(TRG))
                for j, (n, b, off, p) in enumerate(TWOS):
                    if j >= 3:
                        pe.wait_ge(bias_added, i * len(TWOS) + j - 2)
                    for t in range(2):
                        last = nc.tensor.matmul(two(j, p, 3)[:, t, :], gatet[:, b, off + t * p:off + t * p + p], b2_s[:],
                                                start=True, stop=True)
                    last.then_inc(bias_mm, 1)

            pe.wait_ge(emap_ready, ROUNDS)
            turns = (NSLOT - 2 - REST) // UNROLL
            with pe.Fori(0, turns) as q:
                e = [expert(q * UNROLL + REST + d) for d in (-1, 0, 1)]
                for u in range(UNROLL):
                    e = slot_step(q * UNROLL + REST + u, (REST + u) % 2, e, next_e=u < UNROLL - 1)
            first = REST + turns * UNROLL
            e = [expert(first + d) for d in (-1, 0, 1)]
            for s in range(first, NSLOT):
                e = slot_step(s, s % 2, e, next_up=s < NSLOT - 1, next_x=s < NSLOT - 2, next_e=s < NSLOT - 2)
            down(NSLOT - 1, (NSLOT - 1) % 2, e[0])

        @block.vector
        def _(dve):
            V = nc.vector
            steps = [0]

            def link(ins):
                steps[0] += 1
                ins.then_inc(vec, 1)
                dve.wait_ge(vec, steps[0])

            def x_out(s, par, s4=None):
                dve.wait_ge(xh_ready, s + 1)
                if not isinstance(s, int) or s >= 4:
                    dve.wait_ge(y_out[par], 8 * s - 16 - 8 * par)
                if s4 is None:
                    s4 = s % 4
                V.scalar_tensor_tensor(dest[:, s4:s4 + 1], xin[par][:, D + 1:D + 2], emf[:, bass.ds(s, 1)],
                                       xin[par][:, D:D + 1], op0=ALU.is_equal, op1=ALU.add)
                at = par * 256
                V.tensor_tensor(r(xtl[:, par]), bank[4][:, at:at + 128], xth[:, par], op=ALU.subtract)
                V.tensor_tensor(r(xbl[0:DB, par]), bank[4][0:DB, at + 128:at + 256], xbh[0:DB, par],
                                op=ALU.subtract).then_inc(xt_ready, 1)

            def h_out(s, par, first=False):
                dve.wait_ge(ht_mm, s + 1)
                if not first:
                    dve.wait_ge(down_mm, s - 1)
                V.tensor_copy(hidt[par], bank[6][:, 0:H]).then_inc(ht_ready, 1)

            def slot_step(s, par, next_s4=None, next_x=True):
                h_out(s, par, first=isinstance(s, int) and s < 2)
                if next_x:
                    x_out(s + 2, par, next_s4)

            def slot_steps(where, lo=0, hi=None):
                for s in WITHIN[where][lo:hi]:
                    slot_step(s, s % 2)

            V.memset(x3[:, :, 0:1], 0.0)
            V.memset(xbh[DB:DB + 1], 1.0)
            V.memset(slot0[:], 0.0)
            V.memset(psc[:, 0:1], 0.0)
            V.memset(qsc[:, 0:1], 0.0)
            V.memset(sc[:], 0.0)
            V.memset(mv[:], 1.0)
            V.memset(eps_s[:, 0:1], LN_EPS)
            V.memset(eps_s[:, 1:2], RMS_EPS).then_inc(vec_c, 1)
            dve.wait_ge(ids_in, 16)
            link(V.tensor_scalar(idf[:, 0, :], ids_s[:], 0.0, float(VOCAB), op0=ALU.is_lt, op1=ALU.mult))
            link(V.tensor_tensor(idf[:, 1, :], ids_s[:], idf[:, 0, :], op=ALU.add))
            V.tensor_scalar(idc[:], idf[:, 1, :], 0.0, float(VOCAB - 1), op0=ALU.max, op1=ALU.min).then_inc(idc_ready, 1)
            dve.wait_ge(emb_w_in, 16 * 4)
            link(V.tensor_tensor_reduce(out=scr, in0=tokb_s[:], in1=tokb_s[:], scale=1.0, scalar=0.0,
                                        op0=ALU.mult, op1=ALU.add, accum_out=bsq[:, 0:1]))
            V.tensor_scalar_add(bsq[:, 1:2], bsq[:, 0:1], 1.0).then_inc(vec_c, 1)
            b_img = tokb_s[0:NIMG, :]
            for n in range(ROUNDS):
                cols = slice(n * PAIR * NP_, (n + 1) * PAIR * NP_)
                dve.wait_ge(xsq_ready, n + 1)
                V.tensor_reduce(xss[:, cols], xsq[:, :, cols].rearrange("p k c -> p c k"), axis=AX.X, op=ALU.add)\
                    .then_inc(xss_ready, 1)
            for q in range(2 * B):
                dve.wait_ge(img_mm, q + 1)
                V.tensor_copy(mx[0:NIMG, q, :], bank[q % 2][0:NIMG, 0:D + 1]).then_inc(img_sb, 1)
                dve.wait_ge(img_sb, q + 1)
                link(V.tensor_tensor_reduce(out=scr[0:NIMG, :], in0=mx[0:NIMG, q, 0:D], in1=b_img, scale=1.0,
                                            scalar=0.0, op0=ALU.mult, op1=ALU.add, accum_out=st[:, 4, q:q + 1]))
                V.tensor_reduce(st[:, 5, q:q + 1], mx[0:NIMG, q, 0:D], axis=AX.X, op=ALU.max,
                                apply_absolute_value=True)
                if q in (5, 6):
                    for g in range(4 * (q - 5), 4 * (q - 4)):
                        dve.wait_ge(emb_mm, g + 1)
                        at = TXT_T[2 * g]
                        V.tensor_copy(h[:, at:at + 2, :], bank[4 + g % 4][:, 0:2 * D].rearrange(
                            "p (j d) -> p j d", j=2)).then_inc(emb_sb, 1)

            def row(n):
                return st[:, n, :]

            V.tensor_copy(row(0), mx[0:NIMG, :, D]).then_inc(a_vec, 1)
            dve.wait_ge(att_w_in, 16 * 3)
            V.tensor_scalar(unmix[:], chan_s[:], -1.0, 1.0, op0=ALU.mult, op1=ALU.add).then_inc(vec_c, 1)
            dve.wait_ge(a_act, 1)
            link(V.tensor_scalar_max(st[:, 2:4, :], st[:, 2:4, :], EPS))
            link(V.tensor_scalar_min(row(6), row(2), ZMAX))
            link(V.tensor_scalar(row(7), row(6), -1.0, 1.0, op0=ALU.mult, op1=ALU.add))
            link(V.reciprocal(row(8), row(7)))
            link(V.scalar_tensor_tensor(row(6), row(6), 2.0, row(8), op0=ALU.mult, op1=ALU.mult))
            V.tensor_scalar_add(row(7), row(6), 1.0).then_inc(a_vec, 1)
            dve.wait_ge(a_vec, 2)
            link(V.tensor_scalar_add(row(11), row(7), -1.0))
            link(V.tensor_single_scalar(row(12), row(11), 0.0, op=ALU.is_equal))
            link(V.tensor_tensor(row(11), row(11), row(12), op=ALU.add))
            link(V.reciprocal(row(13), row(11)))
            dve.wait_ge(a_act, 2)
            link(V.tensor_tensor(row(8), row(8), row(12), op=ALU.add))
            link(V.tensor_tensor(row(8), row(8), row(6), op=ALU.mult))
            link(V.tensor_tensor(row(8), row(8), row(13), op=ALU.mult))
            link(V.reciprocal(row(14), row(2)))
            link(V.tensor_tensor(row(14), row(14), row(3), op=ALU.mult))
            V.tensor_tensor(row(9), row(14), row(8), op=ALU.mult).then_inc(a_vec, 1)
            link(V.reciprocal(row(15), row(3)))
            link(V.tensor_single_scalar(row(16), row(5), 0.0, op=ALU.is_gt))
            link(V.tensor_tensor(row(15), row(15), row(16), op=ALU.mult))
            dve.wait_ge(a_act, 3)
            link(V.tensor_tensor(row(15), row(15), row(10), op=ALU.mult))
            link(V.tensor_tensor(row(16), row(15), row(3), op=ALU.mult))
            link(V.tensor_scalar_max(row(16), row(16), EPS))
            link(V.reciprocal(row(17), row(16)))
            link(V.tensor_scalar(row(17), row(17), MAXNORM, 1.0, op0=ALU.mult, op1=ALU.min))
            link(V.tensor_tensor(row(15), row(15), row(17), op=ALU.mult))
            link(V.tensor_tensor(row(16), row(15), row(15), op=ALU.mult))
            link(V.tensor_tensor(row(16), row(16), row(1), op=ALU.mult))
            link(V.tensor_tensor(row(17), row(15), row(4), op=ALU.mult))
            link(V.tensor_scalar(row(18), row(17), 2.0, bsq[0:NIMG, 1:2], op0=ALU.mult, op1=ALU.add))
            link(V.tensor_scalar(row(17), row(17), 2.0, 1.0, op0=ALU.mult, op1=ALU.add))
            link(V.scalar_tensor_tensor(row(17), row(16), bsq[0:NIMG, 0:1], row(17), op0=ALU.mult, op1=ALU.add))
            link(V.tensor_scalar_max(row(17), row(17), EPS))
            link(V.reciprocal(row(19), row(17)))
            link(V.tensor_scalar(row(16), row(16), -1.0, 1.0, op0=ALU.mult, op1=ALU.add))
            link(V.tensor_tensor(row(16), row(16), row(19), op=ALU.mult))
            link(V.tensor_tensor(row(18), row(18), row(15), op=ALU.mult))
            link(V.tensor_tensor(row(18), row(18), row(19), op=ALU.mult))
            for q, (g, _) in enumerate(IMG_T):
                last = V.tensor_scalar(h[0:NIMG, g, :], b_img, st[:, 16, q:q + 1], None, op0=ALU.mult)
            link(last)
            for q, (g, _) in enumerate(IMG_T):
                last = V.scalar_tensor_tensor(h[0:NIMG, g, :], mx[0:NIMG, q, 0:D], st[:, 18, q:q + 1],
                                              h[0:NIMG, g, :], op0=ALU.mult, op1=ALU.add)
                last.then_inc(sum_ready, 1)
            dve.wait_ge(rms_ready, 1)
            link(V.reciprocal(rin[:], rin[:]))

            def scale_words(i):
                for j in range(i * PAIR * 4, (i + 1) * PAIR * 4):
                    g = TXT_T[j]
                    last = V.scalar_tensor_tensor(h[:, g, :], h[:, g, :], rin[:, j:j + 1], normw_s[:],
                                                  op0=ALU.mult, op1=ALU.mult)
                return last

            scale_words(0)
            dve.wait_ge(a_act, 4)
            link(V.tensor_scalar_max(row(21), row(21), EPS))
            link(V.reciprocal(row(22), row(21)))
            link(V.tensor_scalar(row(22), row(22), MAXNORM, 1.0, op0=ALU.mult, op1=ALU.min))

            def project_patches(i):
                for q in range(i * PAIR * 2, (i + 1) * PAIR * 2):
                    g = IMG_T[q][0]
                    last = V.tensor_scalar(h[0:NIMG, g, :], h[0:NIMG, g, :], st[:, 22, q:q + 1], None, op0=ALU.mult)
                return last

            link(project_patches(0))
            dve.wait_ge(pool_c, 11 + 2 * PAIR)

            for i in range(ROUNDS):
                within = i == ROUNDS - 1

                def statistics(n, b):
                    these = [(b * NTILE + t, p) for t, (_, p) in enumerate(TILES)]
                    for g, p in these:
                        last = V.bn_stats(bn[0:p, g, :], hr(i, g, p))
                    link(last)
                    for g, p in these:
                        last = V.bn_aggr(mv[0:p, g, :], bn[0:p, g, :])
                    last.then_inc(var_ready, 1)

                def normalize(n, b):
                    dve.wait_ge(std_ready, (i * LN + n) * PAIR + b + 1)
                    link(V.reciprocal(rstd[:, b * NTILE:(b + 1) * NTILE], rstd[:, b * NTILE:(b + 1) * NTILE]))
                    for t, (_, p) in enumerate(TILES):
                        g = b * NTILE + t
                        V.tensor_scalar((nrm, nrm2)[n][0:p, g, 0:D], hr(i, g, p), mv[0:p, g, 0:1], rstd[0:p, g:g + 1],
                                        op0=ALU.subtract, op1=ALU.mult).then_inc(nrm_ready, 1)

                for b in range(PAIR):
                    statistics(0, b)
                for b in range(PAIR):
                    normalize(0, b)
                if i == 0:
                    scale_words(1)
                    link(project_patches(1))
                dve.wait_ge(filler_in, 16 * NCLEAR)
                dve.wait_ge(tr_done, (i * LN + 1) * NG)
                for m in range(3):
                    for l in range(3):
                        n = m * 3 + l
                        dve.wait_ge(z_ready, i * 9 + n + 1)
                        V.scalar_tensor_tensor(xm[:, m, l, :], x3[:, l, 1:T + 1], chan_s[:, 2 + m, l // 2:l // 2 + 1],
                                               zb[n % 2], op0=ALU.mult, op1=ALU.add).then_inc(xm_ready, 1)

                def got(m, l):
                    dve.wait_ge(kvr_ready, i * NKVR + 2 * KVR.index((m, l)) + 2)

                def differences(at):
                    l = LANES[at]
                    k, w, u = kvr[:, 0, l, :], chan_s[:, 0, l // 2:l // 2 + 1], chan_s[:, 1, l // 2:l // 2 + 1]
                    got(0, l)
                    if at:
                        dve.wait_ge(dif_ready, i * 3 + at)
                    link(V.tensor_tensor_scan(osc[:, 1:T + 1], w.to_broadcast([128, T]), k, -1e38,
                                              op0=ALU.add, op1=ALU.max))
                    V.scalar_tensor_tensor(dif[:, 2 * (at % 2), :], osc[:, 0:T], w, k, op0=ALU.add, op1=ALU.subtract)
                    V.scalar_tensor_tensor(dif[:, 2 * (at % 2) + 1, :], k, u, osc[:, 0:T], op0=ALU.add, op1=ALU.subtract)\
                        .then_inc(dif_ready, 1)

                def sums(at, between=lambda: None):
                    l, g, (wkv, old, decay, now) = LANES[at], i * 3 + at, exl[at % 2]
                    got(1, l)
                    if at:
                        dve.wait_ge(ys_ready, g)
                    dve.wait_ge(ex_ready, g * 4 + 2)
                    link(V.tensor_tensor(bv[at % 2], wkv, kvr[:, 1, l, :], op=ALU.mult))
                    V.tensor_tensor_scan(psc[:, 1:T + 1], decay, bv[at % 2], 0.0, op0=ALU.mult, op1=ALU.add).then_inc(psc_ready, 1)
                    link(V.tensor_tensor_scan(qsc[:, 1:T + 1], decay, wkv, 0.0, op0=ALU.mult, op1=ALU.add))
                    between()
                    dve.wait_ge(ex_ready, g * 4 + 3)
                    link(V.tensor_tensor(den[at % 2], old, qsc[:, 0:T], op=ALU.mult))
                    dve.wait_ge(ex_ready, g * 4 + 4)
                    link(V.tensor_tensor(den[at % 2], den[at % 2], now, op=ALU.add))
                    between()
                    got(2, l)
                    link(V.scalar_tensor_tensor(den[at % 2], kvr[:, 2, l, :], 1.0, den[at % 2], op0=ALU.add, op1=ALU.mult))
                    between()
                    V.reciprocal(den[at % 2][:, 0:MOVE], den[at % 2][:, 0:MOVE])
                    between()
                    link(V.reciprocal(den[at % 2][:, MOVE:T], den[at % 2][:, MOVE:T]))
                    dve.wait_ge(num_ready, g + 1)
                    V.tensor_tensor(ys[:, l, :], num[at % 2], den[at % 2], op=ALU.mult).then_inc(ys_ready, 1)
                    between()

                link(V.memset(osc[:, 0:1], -1e38))
                differences(0)
                differences(1)
                sums(0)
                differences(2)
                dve.wait_ge(dif_ready, (i + 1) * 3)
                V.memset(osc[:, 0:1], 0.0)
                if within:
                    P1, P2 = 1, 1
                    todo = [lambda: None] * P1 + [lambda: (x_out(0, 0), x_out(1, 1))]
                    todo += [lambda: None] * P2 + [lambda: (h_out(0, 0, first=True), x_out(2, 0))]
                    todo += [lambda n=n: slot_steps("sums", n, n + 1) for n in range(len(WITHIN["sums"]))]
                    sums(1, between=lambda: todo.pop(0)() if todo else None)
                    sums(2, between=lambda: todo.pop(0)() if todo else None)
                    while todo:
                        todo.pop(0)()
                else:
                    sums(1)
                    sums(2)
                for b in range(PAIR):
                    for j in range(3 * b, 3 * b + 3):
                        n, _, _, p = TWOS[j]
                        dve.wait_ge(o_mm, i * len(TWOS) + j + 1)
                        V.tensor_tensor(h_two(i, n, p), two(j, p, 4), h_two(i, n, p), op=ALU.add).then_inc(o_added, 1)
                    dve.wait_ge(o_added, i * len(TWOS) + 3 * b + 3)
                    if b == 0:
                        statistics(1, 0)
                if i:
                    dve.wait_ge(scattered, i * 16 * NYG)
                normalize(1, 0)
                statistics(1, 1)
                normalize(1, 1)
                if i == 0:
                    dve.wait_ge(w1_in, 16 * 2)
                    V.tensor_copy(r(w1ah[:]), w1raw[0])
                    link(V.tensor_copy(r(w1bh[:]), w1raw[1][0:DB + 1]))
                    V.tensor_tensor(r(w1al[:]), w1raw[0], w1ah[:], op=ALU.subtract)
                    V.tensor_tensor(r(w1bl[:]), w1raw[1][0:DB + 1], w1bh[:], op=ALU.subtract).then_inc(split_ready, 1)
                if within:
                    slot_steps("project")
                    slot_steps("norm")
                dve.wait_ge(gate_mm, i + 1)
                for b in range(PAIR):
                    for p, t0, t1 in ((NIMG, 0, 2), (128, 2, NTILE)):
                        n0, n1 = b * NTILE + t0, b * NTILE + t1
                        last = V.tensor_copy(sc[0:p, n0:n1, :], bank[3][0:p, E * n0:E * n1].rearrange(
                            "p (n e) -> p n e", e=E))
                link(last)
                for n in range(NALL):
                    last = V.max(m8[:, n, :], sc[:, n, :])
                link(last)
                for n in range(NALL):
                    last = V.max_index(i8[:, n, :], m8[:, n, :], sc[:, n, :])
                V.tensor_tensor(pr[:, 0, :], m8[:, :, 1], m8[:, :, 0], op=ALU.subtract).then_inc(gap_ready, 1)
                link(last)
                link(V.tensor_copy(ixf[:], i8[:, :, 0:2]))
                both = [128, E, NALL]
                for s in range(K):
                    link(V.tensor_tensor(oh[:, s], ixf[:, :, s].rearrange("p (o n) -> p o n", o=1).to_broadcast(both),
                                         eiota[:].rearrange("p (e o) -> p e o", o=1).to_broadcast(both), op=ALU.is_equal))
                link(V.tensor_tensor(rmask[:], oh[:, 0], oh[:, 1], op=ALU.add))
                V.tensor_tensor(rmask[:], rmask[:], vmask[:].rearrange("p (o n) -> p o n", o=1).to_broadcast(both),
                                op=ALU.mult).then_inc(mask_ready, 1)
                if within:
                    slot_steps("gate")
                dve.wait_ge(e2_ready, i + 1)
                link(V.tensor_scalar_add(pr[:, 2, :], pr[:, 1, :], 1.0))
                link(V.reciprocal(pr[:, 2, :], pr[:, 2, :]))
                link(V.tensor_tensor(pr[:, 3, :], pr[:, 1, :], pr[:, 2, :], op=ALU.mult))
                for s in range(K):
                    link(V.tensor_tensor(ohw[:, s], oh[:, s],
                                         pr[:, 2 + s, :].rearrange("p (o n) -> p o n", o=1).to_broadcast(both), op=ALU.mult))
                V.tensor_tensor(gate[:].rearrange("p n e -> p e n"), ohw[:, 0], ohw[:, 1], op=ALU.add)\
                    .then_inc(gate_ready, 1)
                V.tensor_copy(prob_all[:, i], pr[:, 2:4, :])
                dve.wait_ge(rank_mm, i + 1)

                def flat(ap):
                    return ap.rearrange("p e n -> p (e n)")

                total, sums_, slot, prod = (cnt[:, n] for n in range(4))
                link(V.tensor_copy(flat(total), bank[3][:, E * NALL:2 * E * NALL]))
                link(V.tensor_tensor_scan(flat(sums_), ones[:].to_broadcast([128, E * NALL]), flat(total), 0.0,
                                          op0=ALU.mult, op1=ALU.add))
                link(V.tensor_tensor(sums_, sums_, total, op=ALU.subtract))
                link(V.tensor_reduce(per_e[:, 0, :], total, axis=AX.X, op=ALU.add))
                over_s = [128, E, EXP_TILES]
                link(V.tensor_tensor(over[:], per_e[:, 0, :].rearrange("p (e o) -> p e o", o=1).to_broadcast(over_s),
                                     thr[:].rearrange("p (o j) -> p o j", o=1).to_broadcast(over_s), op=ALU.is_gt))
                link(V.tensor_reduce(per_e[:, 1, :], over[:], axis=AX.X, op=ALU.add))
                link(V.tensor_tensor_scan(per_e[:, 2, :], ones[:].to_broadcast([128, E]), per_e[:, 1, :], 0.0,
                                          op0=ALU.mult, op1=ALU.add))
                link(V.tensor_tensor(per_e[:, 3, :], per_e[:, 2, :], per_e[:, 1, :], op=ALU.subtract))
                link(V.scalar_tensor_tensor(per_e[:, 4, :], per_e[:, 3, :], 128.0, sums_[:, :, 0],
                                            op0=ALU.mult, op1=ALU.subtract))
                link(V.tensor_scalar(per_e[:, 4, :], per_e[:, 4, :], slot0[:], None, op0=ALU.add))
                link(V.tensor_tensor(flat(slot), flat(sums_), bank[3][:, 0:E * NALL], op=ALU.add))
                link(V.tensor_tensor(slot, slot, per_e[:, 4, :].rearrange("p (e o) -> p e o", o=1).to_broadcast(both),
                                     op=ALU.add))
                for k in range(K):
                    link(V.tensor_tensor(prod, slot, oh[:, k], op=ALU.mult))
                    link(V.tensor_reduce(posf[:, k, :], prod.rearrange("p e n -> p n e"), axis=AX.X, op=ALU.add))
                V.tensor_scalar_add(nrm2[:, :, D], place[:], float(K * PAIR * T * i))
                V.tensor_copy(nrm2[:, :, D + 1], ixf[:, :, 0])
                V.tensor_copy(pos[:, i, :], posf.rearrange("p k n -> p (k n)")).then_inc(pos_ready, 1)
                le_s = [128, SLOT_TILES, E]
                link(V.tensor_tensor(le, per_e[:, 2, :].rearrange("p (o e) -> p o e", o=1).to_broadcast(le_s),
                                     siota[:].rearrange("p (s o) -> p s o", o=1).to_broadcast(le_s), op=ALU.is_le))
                these = slice(i * SLOT_TILES, (i + 1) * SLOT_TILES)
                link(V.tensor_reduce(emf[:, these], le, axis=AX.X, op=ALU.add))
                V.tensor_scalar_min(emap[:, these], emf[0:1, these], float(E - 1)).then_inc(emap_ready, 1)
                link(V.tensor_scalar_add(slot0[:], slot0[:], float(SLOT_TILES * 128)))
                if within:
                    slot_steps("route")
                for j, (n, b, off, p) in enumerate(TWOS):
                    dve.wait_ge(bias_mm, i * len(TWOS) + j + 1)
                    V.tensor_tensor(h_two(i, n, p), two(j, p, 3), h_two(i, n, p), op=ALU.add).then_inc(bias_added, 1)
                dve.wait_ge(bias_added, (i + 1) * len(TWOS))

            def add_answers(i, k, b):
                dve.wait_ge(answers_in[i][b], 16 * 2)
                for t in range(NTILE):
                    n, p = b * NTILE + t, TILES[t][1]
                    if k:
                        dve.wait_ge(y_added, (i * PAIR + b) * K * NTILE + NTILE)
                    V.scalar_tensor_tensor(hr(i, n, p), yg[i][0:p, n, K - 1 - k, :], prob_all[0:p, i, k, n:n + 1],
                                           hr(i, n, p), op0=ALU.mult, op1=ALU.add).then_inc(y_added, 1)

            def finish(i):
                dve.wait_ge(y_added, (i + 1) * K * NALL)
                V.memset(slot0[:], 0.0).then_inc(h_final, 1)

            def slot_loop(lo, hi):
                turns = (hi - lo) // 8
                if turns:
                    with dve.Fori(0, turns) as q:
                        for u in range(8):
                            slot_step(q * 8 + lo + u, (lo + u) % 2, (lo + u + 2) % 4)
                for s in range(lo + 8 * turns, hi):
                    slot_step(s, s % 2)

            at = REST
            for n, s in enumerate((ADD_AT, ADD_AT + 2, ADD_AT + 4, ADD_AT + 6)):
                slot_loop(at, s)
                at = s
                add_answers(0, n % K, n // K)
            finish(0)
            slot_loop(at, NSLOT - 2)
            slot_step(NSLOT - 2, 0, next_x=False)
            slot_step(NSLOT - 1, 1, next_x=False)
            for n in range(K * PAIR):
                add_answers(ROUNDS - 1, n % K, n // K)
            finish(ROUNDS - 1)


_INS = [("xp", (128, KP, B * NP_)), ("tokw", (128, KP, D)), ("tokb", (D,)), ("ids", (128, B * 4)),
        ("basin", (VOCAB, BASIN)), ("projt", (BASIN, D)), ("normw", (D,)), ("chan", (128, 5, 2)),
        ("attwa", (128, 4, D)), ("attwb", (128, 4, D)), ("w1a", (DA, E, H)), ("w1b", (DB + 1, E, H)),
        ("w2", (128, E, KH, D)), ("b2", (E, D)), ("wga", (DA, E)), ("wgb", (DB, E))]


def kernel(x, x_txt, L0_tok_W, L0_tok_b, L0_txt_basin_coords, L0_txt_proj_w, L0_txt_norm_w,
           L0_attn_time_decay, L0_attn_time_first, L0_attn_time_mix_k, L0_attn_time_mix_v, L0_attn_time_mix_r,
           L0_attn_Wk, L0_attn_Wv, L0_attn_Wr, L0_attn_Wo,
           L0_ffn_Wg, L0_ffn_W1, L0_ffn_b1, L0_ffn_W2, L0_ffn_b2):
    import numpy as np
    import concourse.bacc as bacc
    from concourse.bass_utils import run_bass_kernel_spmd

    side = HW // PATCH
    pix = np.asarray(x).reshape(B, CH, side, PATCH, side, PATCH).transpose(1, 3, 5, 0, 2, 4).reshape(KP, 128, B * NP_)
    chan = [np.asarray(a).reshape(D) for a in (L0_attn_time_decay, L0_attn_time_first, L0_attn_time_mix_k,
                                               L0_attn_time_mix_v, L0_attn_time_mix_r)]
    att = np.stack([np.asarray(a).T for a in (L0_attn_Wk, L0_attn_Wv, L0_attn_Wr, L0_attn_Wo)], axis=1)
    w1, w2, wg = np.asarray(L0_ffn_W1), np.asarray(L0_ffn_W2), np.asarray(L0_ffn_Wg)
    data = {
        "xp": pix.transpose(1, 0, 2),
        "tokw": np.asarray(L0_tok_W).T.reshape(KP, 128, D).transpose(1, 0, 2),
        "tokb": np.asarray(L0_tok_b),
        "ids": np.asarray(x_txt).reshape(B * 4, 128).T,
        "basin": np.asarray(L0_txt_basin_coords),
        "projt": np.asarray(L0_txt_proj_w).T,
        "normw": np.asarray(L0_txt_norm_w),
        "chan": np.stack([np.stack([a[:DA], np.concatenate([a[DA:], a[DA:]])], axis=1) for a in chan], axis=1),
        "attwa": att[:DA], "attwb": np.concatenate([att[DA:], att[DA:]]),
        "w1a": w1[:, :DA].transpose(1, 0, 2), 
        "w1b": np.concatenate([w1[:, DA:], np.asarray(L0_ffn_b1)[:, None]], axis=1).transpose(1, 0, 2),
        "w2": w2.reshape(E, KH, 128, D).transpose(2, 0, 1, 3),
        "b2": np.asarray(L0_ffn_b2),
        "wga": wg[:DA], "wgb": wg[DA:],
    }
    nc = bacc.Bacc("TRN2", target_bir_lowering=False, num_devices=1)
    arrays, args = {}, []
    for name, shape in _INS:
        a = np.ascontiguousarray(data[name])
        assert a.shape == shape, (name, a.shape)
        arrays[name] = a
        args.append(nc.dram_tensor(name, a.shape, mybir.dt.from_np(a.dtype), kind="ExternalInput").ap())
    args.append(nc.dram_tensor("out", (B, T, D), mybir.dt.float32, kind="ExternalOutput").ap())
    for name, shape in (("slot_x", (SLOTS, ROW)), ("answers", (K * B * T, D))):
        args.append(nc.dram_tensor(name, shape, mybir.dt.float32, kind="Internal").ap())
    build(nc, *args)
    r = run_bass_kernel_spmd(nc, [arrays], core_ids=[0])
    return r.results[0]["out"]
```
